# Optimizing a Trainium2 kernel written in Bass

```python
import numpy as np
import jax
import jax.numpy as jnp

def _softmax(x, axis=-1):
    return jax.nn.softmax(x, axis=axis)

def _gelu(x):
    return jax.nn.gelu(x, approximate=True)

def _silu(x):
    return jax.nn.silu(x)

def _sigmoid(x):
    return jax.nn.sigmoid(x)

def _layernorm(x, axis=-1, eps=1e-05):
    m = jnp.mean(x, axis=axis, keepdims=True)
    v = jnp.var(x, axis=axis, keepdims=True)
    return (x - m) / jnp.sqrt(v + eps)

def _scatter_add(tgt, idx, src, axis=0):
    return tgt.at[idx].add(src)

def _segment_sum(src, seg, n):
    return jax.ops.segment_sum(src, seg, n)
kernel_name = 'mk_conv_seq_d1_conv_nchw256_r2_e01132'

def setup_inputs(seed: int=0):
    np.random.seed(seed)
    _w = jnp.asarray

    def _rec_inputs():
        import jax
        import jax.numpy as jnp
        _gk = jax.random.key(seed)
        x = 7.22e-05 + 1 * jax.random.normal(jax.random.fold_in(_gk, 1), (8, 128, 32, 32), jnp.float32)
        return x
    x = _rec_inputs()

    def _L0_conv_setup():
        import jax, jax.numpy as jnp
        import numpy as np
        B, C, CI, H, W = (8, 128, 64, 32, 32)
        key = jax.random.key(seed)
        ks = jax.random.split(key, 8)
        s = 0.05
        return {'x': jax.random.normal(ks[0], (B, C, H, W), dtype=jnp.float32), 'Wq': jax.random.normal(ks[1], (CI, C), dtype=jnp.float32) * s, 'bq': jax.random.normal(ks[2], (CI,), dtype=jnp.float32) * s, 'Wk': jax.random.normal(ks[3], (CI, C), dtype=jnp.float32) * s, 'bk': jax.random.normal(ks[4], (CI,), dtype=jnp.float32) * s, 'Wv': jax.random.normal(ks[5], (C, C), dtype=jnp.float32) * s, 'bv': jax.random.normal(ks[6], (C,), dtype=jnp.float32) * s, 'gamma': jnp.zeros((1,), dtype=jnp.float32) + 0.5}
    _L0_conv_all = _L0_conv_setup()
    _L0_conv_in = {k: v for k, v in _L0_conv_all.items() if k in ('Wq', 'bq', 'Wk', 'bk', 'Wv', 'bv', 'gamma')}
    del _L0_conv_all
    return {'x': x, 'L0_conv_Wq': _L0_conv_in['Wq'], 'L0_conv_bq': _L0_conv_in['bq'], 'L0_conv_Wk': _L0_conv_in['Wk'], 'L0_conv_bk': _L0_conv_in['bk'], 'L0_conv_Wv': _L0_conv_in['Wv'], 'L0_conv_bv': _L0_conv_in['bv'], 'L0_conv_gamma': _L0_conv_in['gamma']}

def reference(x, L0_conv_Wq, L0_conv_bq, L0_conv_Wk, L0_conv_bk, L0_conv_Wv, L0_conv_bv, L0_conv_gamma):
    import jax
    import jax.numpy as jnp

    def _L0_conv_ref(x, Wq, bq, Wk, bk, Wv, bv, gamma):
        import jax, jax.numpy as jnp
        import numpy as np
        B, C, CI, H, W = (8, 128, 64, 32, 32)
        b, c, h, w = x.shape
        n = h * w
        xf = x.reshape(b, c, n)
        q = jnp.einsum('oc,bcn->bon', Wq, xf) + bq[None, :, None]
        k = jnp.einsum('oc,bcn->bon', Wk, xf) + bk[None, :, None]
        v = jnp.einsum('oc,bcn->bon', Wv, xf) + bv[None, :, None]
        attn = jnp.einsum('bci,bcj->bij', q, k)
        attn = jax.nn.softmax(attn, axis=-1)
        out = jnp.einsum('bcn,bmn->bcm', v, attn).reshape(b, c, h, w)
        return gamma * out + x

    def _gn(v, G=32, eps=1e-05):
        B_, C_, H_, W_ = v.shape
        g = v.reshape(B_, G, C_ // G, H_, W_)
        m = jnp.mean(g, axis=(2, 3, 4), keepdims=True)
        s = jnp.var(g, axis=(2, 3, 4), keepdims=True)
        return ((g - m) / jnp.sqrt(s + eps)).reshape(v.shape)

    def _ln_c(v, eps=1e-06):
        m = jnp.mean(v, axis=1, keepdims=True)
        s = jnp.var(v, axis=1, keepdims=True)
        return (v - m) / jnp.sqrt(s + eps)

    def _ln_t(v, eps=1e-05):
        m = jnp.mean(v, axis=-1, keepdims=True)
        s = jnp.var(v, axis=-1, keepdims=True)
        return (v - m) / jnp.sqrt(s + eps)

    def _to_tokens(v):
        B_, C_, H_, W_ = v.shape
        return v.reshape(B_, C_, H_ * W_).transpose(0, 2, 1)

    def _from_tokens(t, like):
        B_, C_, H_, W_ = like.shape
        return t.transpose(0, 2, 1).reshape(B_, C_, H_, W_)
    x = _L0_conv_ref(x, L0_conv_Wq, L0_conv_bq, L0_conv_Wk, L0_conv_bk, L0_conv_Wv, L0_conv_bv, L0_conv_gamma)
    return x

_drawn_inputs = setup_inputs


def setup_inputs(seed=0):
    import zlib

    import numpy as np

    out = dict(_drawn_inputs(seed))
    spreads = {}
    factors = {'L0_conv_bq': 4.162, 'L0_conv_bk': 8.0}
    for name, (base, spread) in spreads.items():
        noise = np.random.default_rng([zlib.crc32(name.encode()), seed]).standard_normal(out[name].shape)
        drawn = base * np.exp(spread * noise) if base else spread * noise
        out[name] = jnp.asarray(drawn.astype(out[name].dtype))
    for name, factor in factors.items():
        out[name] = (out[name] * factor).astype(out[name].dtype)
    return out
```

```python
from collections import namedtuple
from contextlib import ExitStack

import concourse.bass as bass
import concourse.mybir as mybir

BATCHES = 8
CHANNELS = 128
HEAD = 64
PIXELS = 32 * 32
TILE = 128
CHUNK = 512
CHUNKS = PIXELS // CHUNK
TILES = PIXELS // TILE
CHUNK_TILES = CHUNK // TILE
STEPS = CHUNKS * TILES
AHEAD = 2
RING = 4
VCOLS = 2 * CHANNELS + 2
MASK_ROWS = 2
IDENTITY_MADE = 2
SETUP_MADE = 14
WEIGHT_LOADS = 7

JOBS = {
    0: ["v0_next", "mx4"], 1: ["mx5"], 2: ["mx6"], 3: ["mx7"], 4: ["qk_next"], 5: ["mt1"],
    7: ["out_prev"], 8: ["v1_next"], 9: ["mx0_next"], 10: ["mx1_next"], 11: ["mx2_next"],
    12: ["mx3_next"], 13: ["mt0_next"], 14: ["out_this"],
}
PROLOGUE_JOBS = ["qk_next", "v0_next", "v1_next", "mx0_next", "mx1_next", "mx2_next", "mx3_next", "mt0_next"]

BANKS = {"qk": (0, 1), "v0": (0,), "v1": (0,), "mt0": (0,), "mt1": (0,), "out": (1,)}


def banks_of(job):
    return (0, 1) if job.startswith("mx") else BANKS[job.split("_")[0]]


def bank_order(bank, jobs):
    return [j for j in jobs if bank in banks_of(j)]


Batch = namedtuple("Batch", "pair parity")


def index(b):
    return 2 * b.pair + b.parity


def after(b):
    return Batch(b.pair, 1) if b.parity == 0 else Batch(b.pair + 1, 0)


def before(b):
    return Batch(b.pair, 0) if b.parity == 1 else Batch(b.pair - 1, 1)


def over_batches(engine, batch_body):
    batch_body(Batch(0, 0), False, True)
    with engine.Fori(0, BATCHES // 2 - 1) as pair:
        batch_body(Batch(pair, 1), True, True)
        batch_body(Batch(pair + 1, 0), True, True)
    batch_body(Batch(BATCHES // 2 - 1, 1), True, False)


def jobs_of(step, has_prev, has_next):
    return [j for j in JOBS.get(step, []) if (has_prev or j != "out_prev") and (has_next or not j.endswith("_next"))]


def wait(engine, semaphore, count):
    if isinstance(count, int) and count <= 0:
        return
    engine.wait_ge(semaphore, count)


def job_before(bank, job, b, has_prev, has_next):
    prologue = bank_order(bank, PROLOGUE_JOBS)
    if b is None:
        i = prologue.index(job)
        return (prologue[i - 1], None) if i else (None, None)
    order = bank_order(bank, [j for s in range(STEPS) for j in jobs_of(s, has_prev, has_next)])
    i = order.index(job)
    if i:
        return order[i - 1], b
    if not has_prev:
        return prologue[-1], None
    return bank_order(bank, [j for s in range(STEPS) for j in JOBS.get(s, [])])[-1], before(b)


def attention_program(nc, x, Wq, bq, Wk, bk, Wv, bv, gamma, out):
    fp32 = mybir.dt.float32
    fp32r = mybir.dt.float32r
    bf16 = mybir.dt.bfloat16
    ALU = mybir.AluOpType
    ACT = mybir.ActivationFunctionType
    AX = mybir.AxisListType

    x_dram = x.rearrange("b c h w -> b c (h w)")
    out_dram = out.rearrange("b c h w -> b c (h w)")

    with ExitStack() as ctx:
        def sbuf(name, shape, dtype):
            return ctx.enter_context(nc.sbuf_tensor(name, shape, dtype))

        def psum(name, shape, dtype):
            return ctx.enter_context(nc.psum_tensor(name, shape, dtype))

        def sem(name):
            return ctx.enter_context(nc.semaphore(name))

        identity = sbuf("identity", [128, 128], fp32)
        identity_r = sbuf("identity_r", [128, 128], fp32r)
        w_qk = sbuf("w_qk", [2 * HEAD, CHANNELS], fp32)
        w_v = sbuf("w_v", [CHANNELS, CHANNELS], fp32)
        w_qk_t = sbuf("w_qk_t", [CHANNELS, 2 * HEAD], fp32)
        w_v_t = sbuf("w_v_t", [CHANNELS, CHANNELS], fp32)
        b_qk = sbuf("b_qk", [2 * HEAD, 1], fp32)
        b_v = sbuf("b_v", [CHANNELS, 1], fp32)
        gamma_col = sbuf("gamma_col", [128, 1], fp32)
        gamma_bv = sbuf("gamma_bv", [128, 1], fp32)
        x_sb = sbuf("x_sb", [CHANNELS, 2, PIXELS], fp32)
        x_bias = sbuf("x_bias", [CHANNELS, 2, PIXELS], fp32)
        qk_hi = sbuf("qk_hi", [2 * HEAD, PIXELS], fp32r)
        qk_lo = sbuf("qk_lo", [2 * HEAD, PIXELS], fp32r)
        q_hihi = [sbuf(f"q_hihi{p}", [128, PIXELS], fp32r) for p in range(2)]
        k_hilo = [sbuf(f"k_hilo{p}", [128, PIXELS], fp32r) for p in range(2)]
        q_lomax = [sbuf(f"q_lomax{p}", [128, PIXELS], fp32r) for p in range(2)]
        k_hione = [sbuf(f"k_hione{p}", [128, PIXELS], fp32r) for p in range(2)]
        values = [sbuf(f"values{p}", [TILE, TILES, VCOLS], fp32r) for p in range(2)]
        values_b = [sbuf(f"values_b{p}", [TILE, TILES, CHANNELS + 2], bf16) for p in range(2)]
        neg_max = sbuf("neg_max", [TILE, TILES], fp32)
        neg_max_split = sbuf("neg_max_split", [TILE, 2, TILES], fp32r)
        weight = sbuf("weight", [TILE, RING, CHUNK], fp32)
        weight_hi = sbuf("weight_hi", [TILE, RING, CHUNK], fp32r)
        weight_lo = sbuf("weight_lo", [TILE, RING, CHUNK], bf16)
        low_sum = sbuf("low_sum", [TILE, CHUNK_TILES, CHANNELS], fp32)
        total = sbuf("total", [TILE, CHUNK_TILES, CHANNELS], fp32)
        one_over = sbuf("one_over", [TILE, CHUNK_TILES], fp32)
        scaled = sbuf("scaled", [TILE, CHUNK_TILES, CHANNELS], fp32)
        y_sb = sbuf("y_sb", [CHANNELS, CHUNKS, CHUNK], fp32)

        scores = psum("scores", [TILE, 2, CHUNK], fp32)
        sums = psum("sums", [TILE, CHUNK_TILES, CHUNK], fp32)
        work = psum("work", [128, 2 * CHUNK], fp32)

        weights_loaded = sem("weights_loaded")
        x_loaded = [sem(f"x_loaded{p}") for p in range(2)]
        spread_loaded = [sem(f"spread_loaded{p}") for p in range(2)]
        y_stored = [sem(f"y_stored{h}") for h in range(CHUNKS)]
        pool_setup = sem("pool_setup")
        x_bias_done = sem("x_bias_done")
        values_b_done = sem("values_b_done")
        scaled_done = sem("scaled_done")
        w_turned = sem("w_turned")
        qk_done = sem("qk_done")
        v_done = sem("v_done")
        mx_done = sem("mx_done")
        mt_done = sem("mt_done")
        scores_done = sem("scores_done")
        sums_step = sem("sums_step")
        sums_done = sem("sums_done")
        out_turned = sem("out_turned")
        qk_hi_done = sem("qk_hi_done")
        v_hi_done = sem("v_hi_done")
        weight_hi_done = sem("weight_hi_done")
        low_sum_done = sem("low_sum_done")
        max_rows_done = sem("max_rows_done")
        w_ready = sem("w_ready")
        qk_lo_done = sem("qk_lo_done")
        v_lo_done = sem("v_lo_done")
        neg_max_done = sem("neg_max_done")
        neg_max_hi_done = sem("neg_max_hi_done")
        neg_max_split_done = sem("neg_max_split_done")
        weight_lo_done = sem("weight_lo_done")
        sums_freed = sem("sums_freed")
        y_done = sem("y_done")

        block = ctx.enter_context(nc.Block())

        def bank(i):
            return work[:, i * CHUNK:(i + 1) * CHUNK]

        def chunk(h):
            return slice(h * CHUNK, (h + 1) * CHUNK)

        def tile(t):
            return slice(t * TILE, (t + 1) * TILE)

        @block.sync
        def _(sp):
            def image(dram, b):
                n = index(b)
                return dram[n] if isinstance(n, int) else dram[bass.ds(sp.snap(n), 1)].rearrange("b c n -> (b c) n")

            def x_of(b):
                return image(x_dram, b)

            def load_x(b, source):
                sp.dma_start(x_sb[:, b.parity], source).then_inc(x_loaded[b.parity], 16)

            def spread(b):
                p, done = b.parity, spread_loaded[b.parity]
                sp.wait_ge(qk_hi_done, CHUNKS * index(b) + CHUNKS)
                sp.dma_start(q_hihi[p][0:HEAD, :].bitcast(fp32), qk_hi[0:HEAD, :].bitcast(fp32)).then_inc(done, 16)
                sp.dma_start(k_hilo[p][0:HEAD, :].bitcast(fp32), qk_hi[HEAD:2 * HEAD, :].bitcast(fp32)).then_inc(done, 16)
                sp.dma_start(q_hihi[p][HEAD:2 * HEAD, :].bitcast(fp32), qk_hi[0:HEAD, :].bitcast(fp32)).then_inc(done, 16)
                sp.dma_start(k_hione[p][0:HEAD, :].bitcast(fp32), qk_hi[HEAD:2 * HEAD, :].bitcast(fp32)).then_inc(done, 16)
                sp.wait_ge(qk_lo_done, CHUNKS * index(b) + CHUNKS)
                sp.dma_start(k_hilo[p][HEAD:2 * HEAD, :].bitcast(fp32), qk_lo[HEAD:2 * HEAD, :].bitcast(fp32)).then_inc(done, 16)
                sp.dma_start(q_lomax[p][0:HEAD, :].bitcast(fp32), qk_lo[0:HEAD, :].bitcast(fp32)).then_inc(done, 16)

            def store_y(b, h):
                place = image(out_dram, b)
                sp.wait_ge(y_done, CHUNKS * index(b) + h + 1)
                sp.dma_start(place[:, chunk(h)], y_sb[:, h]).then_inc(y_stored[h], 16)

            def batch(b, has_prev, has_next, load):
                if load:
                    source = x_of(after(after(b)))
                    sp.wait_ge(values_b_done, CHUNKS * index(b) + CHUNKS)
                    load_x(after(after(b)), source)
                if has_next:
                    spread(after(b))
                if has_prev:
                    store_y(before(b), 1)
                store_y(b, 0)

            load_x(Batch(0, 0), x_of(Batch(0, 0)))
            sp.dma_start(b_qk[0:HEAD, :], bq.rearrange("(p a) -> p a", a=1)).then_inc(weights_loaded, 16)
            sp.dma_start(b_qk[HEAD:2 * HEAD, :], bk.rearrange("(p a) -> p a", a=1)).then_inc(weights_loaded, 16)
            sp.dma_start(b_v[:, :], bv.rearrange("(p a) -> p a", a=1)).then_inc(weights_loaded, 16)
            sp.dma_start(gamma_col[:, :], gamma.rearrange("(p a) -> p a", a=1).broadcast_to([128, 1])).then_inc(weights_loaded, 16)
            load_x(Batch(0, 1), x_of(Batch(0, 1)))
            spread(Batch(0, 0))
            batch(Batch(0, 0), False, True, True)
            with sp.Fori(0, BATCHES // 2 - 2) as pair:
                batch(Batch(pair, 1), True, True, True)
                batch(Batch(pair + 1, 0), True, True, True)
            batch(Batch(2, 1), True, True, True)
            batch(Batch(3, 0), True, True, False)
            batch(Batch(3, 1), True, False, False)
            store_y(Batch(3, 1), 1)
            for h in range(CHUNKS):
                sp.wait_ge(y_stored[h], 16 * BATCHES)

        @block.gpsimd
        def _(pool):
            pool.memset(identity[:, :], 0.0).then_inc(pool_setup, 1)
            pool.wait_ge(pool_setup, 1)
            pool.affine_select(out=identity[:, :], in_=identity[:, :], compare_op=ALU.not_equal, fill=1.0,
                               base=0, pattern=[[-1, 128]], channel_multiplier=1).then_inc(pool_setup, 1)
            pool.wait_ge(pool_setup, IDENTITY_MADE)
            pool.tensor_scalar(identity_r[:, :], identity[:, :], 0.0, 1.0, ALU.add, ALU.mult).then_inc(pool_setup, 1)
            made = IDENTITY_MADE + 1
            for p in range(2):
                pool.wait_ge(pool_setup, made)
                pool.memset(values[p][:, :, 2 * CHANNELS:VCOLS].bitcast(fp32), 1.0).then_inc(pool_setup, 1)
                pool.memset(values_b[p][:, :, CHANNELS:CHANNELS + 2], 1.0).then_inc(pool_setup, 1)
                pool.wait_ge(pool_setup, made + 2)
                pool.memset(q_lomax[p][HEAD:128, :].bitcast(fp32), 0.0).then_inc(pool_setup, 1)
                pool.memset(k_hione[p][HEAD:128, :].bitcast(fp32), 0.0).then_inc(pool_setup, 1)
                pool.wait_ge(pool_setup, made + 4)
                pool.memset(k_hione[p][HEAD:HEAD + MASK_ROWS, :].bitcast(fp32), 1.0).then_inc(pool_setup, 1)
                made += 5
            pool.wait_ge(pool_setup, made)
            pool.wait_ge(weights_loaded, 16 * WEIGHT_LOADS)
            pool.tensor_scalar(gamma_bv[:, :], b_v[:, :], gamma_col[:, :], 1.0, ALU.mult, ALU.mult).then_inc(pool_setup, 1)
            pool.wait_ge(pool_setup, SETUP_MADE)

            def add_bias(b):
                pool.wait_ge(x_loaded[b.parity], 16 * b.pair + 16)
                wait(pool, y_done, CHUNKS * (index(b) - 1))
                pool.tensor_scalar(x_bias[:, b.parity], x_sb[:, b.parity], gamma_bv[:, :], 1.0,
                                   ALU.add, ALU.mult).then_inc(x_bias_done, 1)

            def round_values(b, half):
                tiles = slice(half * CHUNK_TILES, (half + 1) * CHUNK_TILES)
                pool.wait_ge(v_hi_done, CHUNKS * index(b) + half + 1)
                pool.tensor_scalar(values_b[b.parity][:, tiles, 0:CHANNELS],
                                   values[b.parity][:, tiles, CHANNELS:2 * CHANNELS], 0.0, 1.0,
                                   ALU.add, ALU.mult).then_inc(values_b_done, 1)

            def scale(b, h):
                pool.wait_ge(sums_freed, CHUNKS * index(b) + h + 1)
                wait(pool, out_turned, CHUNKS * index(b) + h)
                for it in range(CHUNK_TILES):
                    last = pool.tensor_scalar(scaled[:, it], total[:, it], one_over[:, it:it + 1], gamma_col[:, :],
                                              ALU.mult, ALU.mult)
                last.then_inc(scaled_done, 1)

            def batch(b, has_prev, has_next):
                if has_next:
                    round_values(after(b), 0)
                if has_prev:
                    scale(before(b), 1)
                if has_next:
                    add_bias(after(b))
                    round_values(after(b), 1)
                scale(b, 0)

            add_bias(Batch(0, 0))
            round_values(Batch(0, 0), 0)
            round_values(Batch(0, 0), 1)
            for n in range(BATCHES):
                batch(Batch(n // 2, n % 2), n > 0, n < BATCHES - 1)
            scale(Batch(BATCHES // 2 - 1, 1), 1)

        @block.tensor
        def _(pe):
            pe.wait_ge(pool_setup, IDENTITY_MADE)
            pe.wait_ge(weights_loaded, 16 * WEIGHT_LOADS)
            pe.transpose(bank(0)[:, 0:128], w_qk[:, :], identity[:, :]).then_inc(w_turned, 1)
            pe.transpose(bank(1)[:, 0:128], w_v[:, :], identity[:, :]).then_inc(w_turned, 1)
            pe.wait_ge(w_ready, 2)

            def wait_read_out(bank_used, job, b):
                n = Batch(0, 0) if b is None else after(b)
                if job is None:
                    pe.wait_ge(w_ready, 2)
                elif job == "qk_next":
                    pe.wait_ge(qk_lo_done, CHUNKS * index(n) + bank_used + 1)
                elif job in ("v0_next", "v1_next"):
                    pe.wait_ge(v_lo_done, CHUNKS * index(n) + int(job[1]) + 1)
                elif job.startswith("mx"):
                    pe.wait_ge(neg_max_done, TILES * index(n if job.endswith("_next") else b) + int(job[2]) + 1)
                elif job.startswith("mt"):
                    pe.wait_ge(max_rows_done, CHUNKS * index(n if job.endswith("_next") else b) + int(job[2]) + 1)
                elif job == "out_prev":
                    pe.wait_ge(y_done, CHUNKS * index(b))
                elif job == "out_this":
                    pe.wait_ge(y_done, CHUNKS * index(b) + 1)

            def take_bank(i, job, b, flags):
                wait_read_out(i, *job_before(i, job, b, *flags))

            def project_qk(n, takes):
                pe.wait_ge(x_loaded[n.parity], 16 * n.pair + 16)
                for h in range(CHUNKS):
                    take_bank(h, "qk_next", *takes)
                    pe.matmul(bank(h), w_qk_t[:, :], x_sb[:, n.parity, chunk(h)], start=True, stop=True).then_inc(qk_done, 1)

            def project_v(n, half, takes):
                pe.wait_ge(x_loaded[n.parity], 16 * n.pair + 16)
                take_bank(0, f"v{half}_next", *takes)
                for t in range(CHUNK_TILES):
                    last = pe.matmul(bank(0)[:, tile(t)], x_sb[:, n.parity, tile(half * CHUNK_TILES + t)], w_v_t[:, :],
                                     start=True, stop=True)
                last.then_inc(v_done, 1)

            def max_scores(n, t, job, takes):
                p = n.parity
                pe.wait_ge(spread_loaded[p], 96 * n.pair + 96)
                for h in range(CHUNKS):
                    if h == 0 or job_before(0, job, takes[0], *takes[1]) != job_before(1, job, takes[0], *takes[1]):
                        take_bank(h, job, *takes)
                    last = pe.matmul(bank(h), q_hihi[p][:, tile(t)], k_hilo[p][:, chunk(h)], start=True, stop=True)
                last.then_inc(mx_done, 1)

            def turn_max(n, h, job, takes):
                pe.wait_ge(neg_max_split_done, CHUNKS * index(n) + h + 1)
                take_bank(0, job, *takes)
                for t in range(CHUNK_TILES):
                    last = pe.transpose(bank(0)[0:2, tile(t)].bitcast(fp32r), neg_max_split[:, :, h * CHUNK_TILES + t],
                                        identity_r[:, :])
                last.then_inc(mt_done, 1)

            def turn_out(n, h, job, takes):
                pe.wait_ge(scaled_done, CHUNKS * index(n) + h + 1)
                take_bank(1, job, *takes)
                for it in range(CHUNK_TILES):
                    last = pe.transpose(bank(1)[:, tile(it)], scaled[:, it], identity[:, :])
                last.then_inc(out_turned, 1)

            def do_job(job, b, n, takes):
                if job == "qk_next":
                    project_qk(n, takes)
                elif job in ("v0_next", "v1_next"):
                    project_v(n, int(job[1]), takes)
                elif job.startswith("mx"):
                    max_scores(n if job.endswith("_next") else b, int(job[2]), job, takes)
                elif job.startswith("mt"):
                    turn_max(n if job.endswith("_next") else b, int(job[2]), job, takes)
                elif job == "out_prev":
                    turn_out(before(b), 1, job, takes)
                elif job == "out_this":
                    turn_out(b, 0, job, takes)

            def score_tile(b, k):
                h, j, p = k // TILES, k % TILES, b.parity
                if k % TILES == 0:
                    pe.wait_ge(max_rows_done, CHUNKS * index(b) + h + 1)
                wait(pe, weight_hi_done, STEPS * index(b) + k - 1)
                pe.matmul(scores[:, k % 2], k_hilo[p][:, tile(j)], q_hihi[p][:, chunk(h)], start=True, stop=False)
                pe.matmul(scores[:, k % 2], k_hione[p][:, tile(j)], q_lomax[p][:, chunk(h)],
                          start=False, stop=True).then_inc(scores_done, 1)

            def weighted_sums(b, k):
                h, j, p, r = k // TILES, k % TILES, b.parity, k % RING
                g = STEPS * index(b) + k
                if j % CHUNK_TILES == 0 and h == 0:
                    half = j // CHUNK_TILES
                    pe.wait_ge(v_lo_done, CHUNKS * index(b) + half + 1)
                    pe.wait_ge(values_b_done, CHUNKS * index(b) + half + 1)
                pe.wait_ge(weight_hi_done, g + 1)
                if j == 0:
                    wait(pe, sums_freed, CHUNKS * index(b) + h)

                def hi(stop):
                    for it in range(CHUNK_TILES):
                        last = pe.matmul(sums[:, it, 0:VCOLS], weight_hi[:, r, tile(it)], values[p][:, j],
                                         start=(j == 0), stop=stop)
                    return last

                def lo():
                    pe.wait_ge(weight_lo_done, g + 1)
                    for it in range(CHUNK_TILES):
                        last = pe.matmul(sums[:, it, CHANNELS:VCOLS], weight_lo[:, r, tile(it)], values_b[p][:, j],
                                         start=False, stop=False)
                    return last

                if j < TILES - 1:
                    hi(False)
                    lo().then_inc(sums_step, 1)
                else:
                    lo().then_inc(sums_step, 1)
                    hi(True).then_inc(sums_done, 1)

            for job in PROLOGUE_JOBS:
                if job == "mt0_next":
                    pe.wait_ge(pool_setup, SETUP_MADE)
                do_job(job, None, Batch(0, 0), (None, (False, False)))
            for k in range(AHEAD):
                score_tile(Batch(0, 0), k)

            def batch(b, has_prev, has_next):
                for k in range(STEPS):
                    if k + AHEAD < STEPS:
                        score_tile(b, k + AHEAD)
                    elif has_next:
                        score_tile(after(b), k + AHEAD - STEPS)
                    for job in jobs_of(k, has_prev, has_next):
                        do_job(job, b, after(b), (b, (has_prev, has_next)))
                    weighted_sums(b, k)

            over_batches(pe, batch)
            last_batch = Batch(BATCHES // 2 - 1, 1)
            pe.wait_ge(scaled_done, CHUNKS * BATCHES)
            wait_read_out(1, "out_this", last_batch)
            for it in range(CHUNK_TILES):
                last = pe.transpose(bank(1)[:, tile(it)], scaled[:, it], identity[:, :])
            last.then_inc(out_turned, 1)

        @block.scalar
        def _(act):
            act.dma_start(w_qk[0:HEAD, :], Wq).then_inc(weights_loaded, 16)
            act.dma_start(w_qk[HEAD:2 * HEAD, :], Wk).then_inc(weights_loaded, 16)
            act.dma_start(w_v[:, :], Wv).then_inc(weights_loaded, 16)
            act.wait_ge(weights_loaded, 16 * WEIGHT_LOADS)

            def round_qk(n):
                for h in range(CHUNKS):
                    act.wait_ge(qk_done, CHUNKS * index(n) + h + 1)
                    if h == 0:
                        m = before(n)
                        if not isinstance(index(n), int) or index(n) > 0:
                            act.wait_ge(spread_loaded[m.parity], 96 * m.pair + 96)
                    act.activation(qk_hi[:, chunk(h)], bank(h), ACT.Identity, bias=b_qk[:, :]).then_inc(qk_hi_done, 1)

            def round_v(n, half):
                act.wait_ge(v_done, CHUNKS * index(n) + half + 1)
                wait(act, sums_step, STEPS * (index(n) - 1))
                act.activation(values[n.parity][:, half * CHUNK_TILES:(half + 1) * CHUNK_TILES, CHANNELS:2 * CHANNELS],
                               bank(0).rearrange("p (t c) -> p t c", c=CHANNELS), ACT.Copy).then_inc(v_hi_done, 1)

            def write_max_rows(n, h):
                act.wait_ge(mt_done, CHUNKS * index(n) + h + 1)
                done = act.activation(q_lomax[n.parity][HEAD:HEAD + MASK_ROWS, chunk(h)], bank(0)[0:2, :], ACT.Copy)
                done.then_inc(max_rows_done, 1)

            def do_job(job, b, n):
                if job == "qk_next":
                    round_qk(n)
                elif job in ("v0_next", "v1_next"):
                    round_v(n, int(job[1]))
                elif job.startswith("mt"):
                    write_max_rows(n if job.endswith("_next") else b, int(job[2]))

            def exponentials(b, k):
                g, r = STEPS * index(b) + k, k % RING
                act.wait_ge(scores_done, g + 1)
                wait(act, weight_lo_done, g - RING + 1)
                act.activation(weight[:, r], scores[:, k % 2], ACT.Exp)
                wait(act, sums_step, g - RING + 1)
                act.activation(weight_hi[:, r], scores[:, k % 2], ACT.Exp).then_inc(weight_hi_done, 1)

            def take_low_sum(b, h):
                c = CHUNKS * index(b) + h
                act.wait_ge(sums_done, c + 1)
                wait(act, sums_freed, c)
                act.activation(low_sum[:, :, :], sums[:, :, 0:CHANNELS], ACT.Copy).then_inc(low_sum_done, 1)

            for job in PROLOGUE_JOBS:
                if job == "mt0_next":
                    act.wait_ge(pool_setup, SETUP_MADE)
                do_job(job, None, Batch(0, 0))
            for k in range(AHEAD):
                exponentials(Batch(0, 0), k)

            def batch(b, has_prev, has_next):
                for k in range(STEPS):
                    if k == 0 and has_prev:
                        take_low_sum(before(b), 1)
                    if k == TILES:
                        take_low_sum(b, 0)
                    if k + AHEAD < STEPS:
                        exponentials(b, k + AHEAD)
                    elif has_next:
                        exponentials(after(b), k + AHEAD - STEPS)
                    for job in jobs_of(k, has_prev, has_next):
                        do_job(job, b, after(b))

            over_batches(act, batch)
            take_low_sum(Batch(BATCHES // 2 - 1, 1), 1)

        @block.vector
        def _(dve):
            for i, w in enumerate((w_qk_t, w_v_t)):
                dve.wait_ge(w_turned, i + 1)
                done = dve.tensor_copy(w[:, :], bank(i)[:, 0:128])
                done.then_inc(w_ready, 1)
            dve.wait_ge(weights_loaded, 16 * WEIGHT_LOADS)

            def rest_of_qk(n):
                for h in range(CHUNKS):
                    dve.wait_ge(qk_hi_done, CHUNKS * index(n) + h + 1)
                    done = dve.scalar_tensor_tensor(qk_lo[:, chunk(h)], bank(h), b_qk[:, :], qk_hi[:, chunk(h)],
                                                    ALU.add, ALU.subtract)
                    done.then_inc(qk_lo_done, 1)

            def rest_of_v(n, half):
                tiles = slice(half * CHUNK_TILES, (half + 1) * CHUNK_TILES)
                dve.wait_ge(v_hi_done, CHUNKS * index(n) + half + 1)
                done = dve.tensor_tensor(values[n.parity][:, tiles, 0:CHANNELS],
                                         bank(0).rearrange("p (t c) -> p t c", c=CHANNELS),
                                         values[n.parity][:, tiles, CHANNELS:2 * CHANNELS], ALU.subtract)
                done.then_inc(v_lo_done, 1)

            def maximum(n, t):
                dve.wait_ge(mx_done, TILES * index(n) + t + 1)
                done = dve.reduce_max(neg_max[:, t:t + 1], work[:, :], AX.X, negate=True)
                done.then_inc(neg_max_done, 1)
                if t % CHUNK_TILES == CHUNK_TILES - 1:
                    c = CHUNKS * index(n) + t // CHUNK_TILES
                    cols = slice(t + 1 - CHUNK_TILES, t + 1)
                    dve.wait_ge(neg_max_done, TILES * index(n) + t + 1)
                    wait(dve, mt_done, c - 1)
                    dve.tensor_copy(neg_max_split[:, 0, cols], neg_max[:, cols]).then_inc(neg_max_hi_done, 1)
                    dve.wait_ge(neg_max_hi_done, c + 1)
                    dve.tensor_tensor(neg_max_split[:, 1, cols], neg_max[:, cols], neg_max_split[:, 0, cols],
                                      ALU.subtract).then_inc(neg_max_split_done, 1)

            def finish(n, h):
                c = CHUNKS * index(n) + h
                dve.wait_ge(out_turned, c + 1)
                dve.wait_ge(x_bias_done, index(n) + 1)
                wait(dve, y_stored[h], 16 * index(n))
                done = dve.tensor_tensor(y_sb[:, h], bank(1), x_bias[:, n.parity, chunk(h)], ALU.add)
                done.then_inc(y_done, 1)

            def do_job(job, b, n):
                if job == "qk_next":
                    rest_of_qk(n)
                elif job in ("v0_next", "v1_next"):
                    rest_of_v(n, int(job[1]))
                elif job.startswith("mx"):
                    maximum(n if job.endswith("_next") else b, int(job[2]))
                elif job == "out_prev":
                    finish(before(b), 1)
                elif job == "out_this":
                    finish(b, 0)

            def low_weights(b, k):
                g, r = STEPS * index(b) + k, k % RING
                dve.wait_ge(weight_hi_done, g + 1)
                wait(dve, sums_step, g - RING + 1)
                dve.tensor_tensor(weight_lo[:, r], weight[:, r], weight_hi[:, r], ALU.subtract).then_inc(weight_lo_done, 1)

            def add_sums(b, h):
                c = CHUNKS * index(b) + h
                dve.wait_ge(low_sum_done, c + 1)
                wait(dve, scaled_done, c)
                dve.reciprocal(one_over[:, :], sums[:, :, 2 * CHANNELS])
                dve.tensor_tensor(total[:, :, :], sums[:, :, CHANNELS:2 * CHANNELS], low_sum[:, :, :],
                                  ALU.add).then_inc(sums_freed, 1)

            for job in PROLOGUE_JOBS:
                do_job(job, None, Batch(0, 0))
            low_weights(Batch(0, 0), 0)

            def batch(b, has_prev, has_next):
                for k in range(STEPS):
                    if k == 0 and has_prev:
                        add_sums(before(b), 1)
                    if k == TILES:
                        add_sums(b, 0)
                    if k + 1 < STEPS:
                        low_weights(b, k + 1)
                    elif has_next:
                        low_weights(after(b), 0)
                    for job in jobs_of(k, has_prev, has_next):
                        do_job(job, b, after(b))

            over_batches(dve, batch)
            last_batch = Batch(BATCHES // 2 - 1, 1)
            add_sums(last_batch, 1)
            finish(last_batch, 1)


_INS = ["x", "L0_conv_Wq", "L0_conv_bq", "L0_conv_Wk", "L0_conv_bk", "L0_conv_Wv", "L0_conv_bv", "L0_conv_gamma"]
_OUT = (BATCHES, CHANNELS, 32, 32)


def kernel(**inputs):
    import numpy as np
    import concourse.bacc as bacc
    from concourse.bass_utils import run_bass_kernel_spmd

    nc = bacc.Bacc("TRN2", target_bir_lowering=False, num_devices=1)
    arrays, args = {}, []
    for name in _INS:
        a = np.ascontiguousarray(inputs[name])
        arrays[f"in_{name}"] = a
        args.append(nc.dram_tensor(f"in_{name}", a.shape, mybir.dt.from_np(a.dtype), kind="ExternalInput").ap())
    args.append(nc.dram_tensor("out_0", _OUT, mybir.dt.float32, kind="ExternalOutput").ap())
    attention_program(nc, *args)
    result = run_bass_kernel_spmd(nc, [arrays], core_ids=[0])
    return result.results[0]["out_0"]
```

```python
from collections import namedtuple
from contextlib import ExitStack

import concourse.bass as bass
import concourse.mybir as mybir

BATCHES = 8
CHANNELS = 128
HEAD = 64
PIXELS = 32 * 32
TILE = 128
CHUNK = 512
CHUNKS = PIXELS // CHUNK
TILES = PIXELS // TILE
CHUNK_TILES = CHUNK // TILE
STEPS = CHUNKS * TILES
AHEAD = 2
HALVES = 2
HALF_TILES = CHUNK_TILES // HALVES
RING = 4
VCOLS = 2 * CHANNELS + 2
IDENTITY_MADE = 2
SETUP_MADE = 14
WEIGHT_LOADS = 7

JOBS = {
    0: (["mx4a", "mx4b"], []),
    1: (["mx5a"], ["mx5b"]),
    2: (["mx6a"], ["mx6b"]),
    3: (["mx7a", "mx7b"], []),
    4: ([], ["qk_next"]),
    5: (["mt1"], []),
    6: (["v0_next"], []),
    7: (["out_prev"], []),
    8: ([], []),
    9: (["mx0a_next"], ["mx0b_next"]),
    10: (["mx1a_next"], ["mx1b_next"]),
    11: (["mx2a_next"], ["mx2b_next"]),
    12: (["mx3a_next", "mx3b_next"], []),
    13: ([], ["mt0_next"]),
    14: (["v1_next"], []),
    15: (["out_this"], []),
}
PROLOGUE_JOBS = ["qk_next", "v0_next", "v1_next", "mx0a_next", "mx0b_next", "mx1a_next", "mx1b_next",
                 "mx2a_next", "mx2b_next", "mx3a_next", "mx3b_next", "mt0_next"]
POOL_STEPS = (1, 2, 3, 4, 10, 11, 12, 13)
SPREAD_MX, SPREAD_REST = 4 * 16, 2 * 16

BANKS = {"qk": (0, 1), "v0": (0,), "v1": (0,), "mt0": (0,), "mt1": (0,), "out": (1,)}


def banks_of(job):
    return ("ab".index(job[3]),) if job.startswith("mx") else BANKS[job.split("_")[0]]


def bank_order(bank, jobs):
    return [j for j in jobs if bank in banks_of(j)]


Batch = namedtuple("Batch", "pair parity")


def index(b):
    return 2 * b.pair + b.parity


def after(b):
    return Batch(b.pair, 1) if b.parity == 0 else Batch(b.pair + 1, 0)


def before(b):
    return Batch(b.pair, 0) if b.parity == 1 else Batch(b.pair - 1, 1)


def over_batches(engine, batch_body):
    batch_body(Batch(0, 0), False, True)
    with engine.Fori(0, BATCHES // 2 - 1) as pair:
        batch_body(Batch(pair, 1), True, True)
        batch_body(Batch(pair + 1, 0), True, True)
    batch_body(Batch(BATCHES // 2 - 1, 1), True, False)


def lo_count(b, k):
    mine = [i for i in range(STEPS) if (i in POOL_STEPS) == (k in POOL_STEPS)]
    return len(mine) * index(b) + mine.index(k) + 1


def mx_count(b, job):
    return 2 * TILES * index(b) + 2 * int(job[2]) + "ab".index(job[3]) + 1


def jobs_of(step, has_prev, has_next):
    return [[j for j in jobs if (has_prev or j != "out_prev") and (has_next or not j.endswith("_next"))]
            for jobs in JOBS[step]]


def all_jobs(has_prev, has_next):
    return [j for step in range(STEPS) for jobs in jobs_of(step, has_prev, has_next) for j in jobs]


def wait(engine, semaphore, count):
    if isinstance(count, int) and count <= 0:
        return
    engine.wait_ge(semaphore, count)


def job_before(bank, job, b, has_prev, has_next):
    prologue = bank_order(bank, PROLOGUE_JOBS)
    if b is None:
        i = prologue.index(job)
        return (prologue[i - 1], None) if i else (None, None)
    order = bank_order(bank, all_jobs(has_prev, has_next))
    i = order.index(job)
    if i:
        return order[i - 1], b
    if not has_prev:
        return prologue[-1], None
    return bank_order(bank, all_jobs(True, True))[-1], before(b)


def attention_program(nc, x, Wq, bq, Wk, bk, Wv, bv, gamma, out):
    fp32 = mybir.dt.float32
    fp32r = mybir.dt.float32r
    bf16 = mybir.dt.bfloat16
    ALU = mybir.AluOpType
    ACT = mybir.ActivationFunctionType
    AX = mybir.AxisListType

    x_dram = x.rearrange("b c h w -> b c (h w)")
    out_dram = out.rearrange("b c h w -> b c (h w)")

    with ExitStack() as ctx:
        def sbuf(name, shape, dtype):
            return ctx.enter_context(nc.sbuf_tensor(name, shape, dtype))

        def psum(name, shape, dtype):
            return ctx.enter_context(nc.psum_tensor(name, shape, dtype))

        def sem(name):
            return ctx.enter_context(nc.semaphore(name))

        identity = sbuf("identity", [128, 128], fp32)
        identity_r = sbuf("identity_r", [128, 128], fp32r)
        w_qk = sbuf("w_qk", [2 * HEAD, CHANNELS], fp32)
        w_v = sbuf("w_v", [CHANNELS, CHANNELS], fp32)
        w_qk_t = sbuf("w_qk_t", [CHANNELS, 2 * HEAD], fp32)
        w_v_t = sbuf("w_v_t", [CHANNELS, CHANNELS], fp32)
        b_qk = sbuf("b_qk", [2 * HEAD, 1], fp32)
        b_v = sbuf("b_v", [CHANNELS, 1], fp32)
        gamma_col = sbuf("gamma_col", [128, 1], fp32)
        gamma_bv = sbuf("gamma_bv", [128, 1], fp32)
        x_sb = sbuf("x_sb", [CHANNELS, 2, PIXELS], fp32)
        x_bias = sbuf("x_bias", [CHANNELS, 2, PIXELS], fp32)
        v_full = sbuf("v_full", [TILE, 2, CHUNK_TILES, CHANNELS], fp32)
        qk_hi = sbuf("qk_hi", [2 * HEAD, PIXELS], fp32r)
        qk_lo = sbuf("qk_lo", [2 * HEAD, PIXELS], fp32r)
        q_hihi = [sbuf(f"q_hihi{p}", [128, PIXELS], fp32r) for p in range(2)]
        k_hilo = [sbuf(f"k_hilo{p}", [128, PIXELS], fp32r) for p in range(2)]
        q_lomax = [sbuf(f"q_lomax{p}", [128, PIXELS], fp32r) for p in range(2)]
        k_hione = [sbuf(f"k_hione{p}", [128, PIXELS], fp32r) for p in range(2)]
        values = [sbuf(f"values{p}", [TILE, TILES, VCOLS], fp32r) for p in range(2)]
        values_b = [sbuf(f"values_b{p}", [TILE, TILES, CHANNELS + 2], bf16) for p in range(2)]
        neg_max = sbuf("neg_max", [TILE, 2, TILES], fp32)
        neg_max_r = sbuf("neg_max_r", [TILE, TILES], fp32r)
        weight = sbuf("weight", [TILE, RING, CHUNK], fp32)
        weight_hi = sbuf("weight_hi", [TILE, RING, CHUNK], fp32r)
        weight_lo = sbuf("weight_lo", [TILE, RING, CHUNK], bf16)
        low_sum = sbuf("low_sum", [TILE, CHUNK_TILES, CHANNELS], fp32)
        total = sbuf("total", [TILE, CHUNK_TILES, CHANNELS], fp32)
        one_over = sbuf("one_over", [TILE, CHUNK_TILES], fp32)
        scaled = sbuf("scaled", [TILE, CHUNK_TILES, CHANNELS], fp32)
        y_sb = sbuf("y_sb", [CHANNELS, CHUNKS, CHUNK], fp32)

        scores = psum("scores", [TILE, 2, CHUNK], fp32)
        sums = psum("sums", [TILE, CHUNK_TILES, CHUNK], fp32)
        work = psum("work", [128, 2 * CHUNK], fp32)

        weights_loaded = sem("weights_loaded")
        x_loaded = [sem(f"x_loaded{p}") for p in range(2)]
        spread_mx = [sem(f"spread_mx{p}") for p in range(2)]
        spread_rest = [sem(f"spread_rest{p}") for p in range(2)]
        y_stored = [sem(f"y_stored{h}") for h in range(CHUNKS)]
        pool_setup = sem("pool_setup")
        x_bias_done = sem("x_bias_done")
        v_hi_done = sem("v_hi_done")
        v_lo_done = sem("v_lo_done")
        values_b_done = sem("values_b_done")
        weight_lo_pool_done = sem("weight_lo_pool_done")
        scaled_done = sem("scaled_done")
        w_turned = sem("w_turned")
        qk_done = sem("qk_done")
        v_done = sem("v_done")
        mx_done = sem("mx_done")
        mt_done = sem("mt_done")
        scores_done = sem("scores_done")
        sums_step = sem("sums_step")
        sums_done = sem("sums_done")
        out_turned = sem("out_turned")
        qk_hi_done = sem("qk_hi_done")
        v_full_done = sem("v_full_done")
        weight_hi_done = sem("weight_hi_done")
        low_sum_done = sem("low_sum_done")
        max_rows_done = sem("max_rows_done")
        w_ready = sem("w_ready")
        qk_lo_done = sem("qk_lo_done")
        neg_max_done = sem("neg_max_done")
        neg_max_r_done = sem("neg_max_r_done")
        weight_lo_done = sem("weight_lo_done")
        sums_freed = sem("sums_freed")
        y_done = sem("y_done")

        block = ctx.enter_context(nc.Block())

        def bank(i):
            return work[:, i * CHUNK:(i + 1) * CHUNK]

        def chunk(h):
            return slice(h * CHUNK, (h + 1) * CHUNK)

        def tile(t):
            return slice(t * TILE, (t + 1) * TILE)

        @block.sync
        def _(sp):
            def image(dram, b):
                n = index(b)
                return dram[n] if isinstance(n, int) else dram[bass.ds(sp.snap(n), 1)].rearrange("b c n -> (b c) n")

            def x_of(b):
                return image(x_dram, b)

            def load_x(b, source):
                sp.dma_start(x_sb[:, b.parity], source).then_inc(x_loaded[b.parity], 16)

            def spread(b):
                p = b.parity
                sp.wait_ge(qk_hi_done, CHUNKS * index(b) + CHUNKS)
                sp.dma_start(k_hilo[p][0:HEAD, :].bitcast(fp32), qk_hi[HEAD:2 * HEAD, :].bitcast(fp32)).then_inc(spread_mx[p], 16)
                sp.dma_start(q_hihi[p][0:HEAD, :].bitcast(fp32), qk_hi[0:HEAD, :].bitcast(fp32)).then_inc(spread_mx[p], 16)
                sp.dma_start(q_hihi[p][HEAD:2 * HEAD, :].bitcast(fp32), qk_hi[0:HEAD, :].bitcast(fp32)).then_inc(spread_mx[p], 16)
                sp.wait_ge(qk_lo_done, CHUNKS * index(b) + CHUNKS)
                sp.dma_start(k_hilo[p][HEAD:2 * HEAD, :].bitcast(fp32), qk_lo[HEAD:2 * HEAD, :].bitcast(fp32)).then_inc(spread_mx[p], 16)
                sp.dma_start(q_lomax[p][0:HEAD, :].bitcast(fp32), qk_lo[0:HEAD, :].bitcast(fp32)).then_inc(spread_rest[p], 16)
                sp.dma_start(k_hione[p][0:HEAD, :].bitcast(fp32), qk_hi[HEAD:2 * HEAD, :].bitcast(fp32)).then_inc(spread_rest[p], 16)

            def store_y(b, h):
                place = image(out_dram, b)
                sp.wait_ge(y_done, CHUNKS * index(b) + h + 1)
                sp.dma_start(place[:, chunk(h)], y_sb[:, h]).then_inc(y_stored[h], 16)

            def batch(b, has_prev, has_next, load):
                if load:
                    source = x_of(after(after(b)))
                    sp.wait_ge(v_lo_done, CHUNKS * index(b) + CHUNKS)
                    load_x(after(after(b)), source)
                if has_next:
                    spread(after(b))
                if has_prev:
                    store_y(before(b), 1)
                store_y(b, 0)

            load_x(Batch(0, 0), x_of(Batch(0, 0)))
            sp.dma_start(b_qk[0:HEAD, :], bq.rearrange("(p a) -> p a", a=1)).then_inc(weights_loaded, 16)
            sp.dma_start(b_qk[HEAD:2 * HEAD, :], bk.rearrange("(p a) -> p a", a=1)).then_inc(weights_loaded, 16)
            sp.dma_start(b_v[:, :], bv.rearrange("(p a) -> p a", a=1)).then_inc(weights_loaded, 16)
            sp.dma_start(gamma_col[:, :], gamma.rearrange("(p a) -> p a", a=1).broadcast_to([128, 1])).then_inc(weights_loaded, 16)
            load_x(Batch(0, 1), x_of(Batch(0, 1)))
            spread(Batch(0, 0))
            batch(Batch(0, 0), False, True, True)
            with sp.Fori(0, BATCHES // 2 - 2) as pair:
                batch(Batch(pair, 1), True, True, True)
                batch(Batch(pair + 1, 0), True, True, True)
            batch(Batch(2, 1), True, True, True)
            batch(Batch(3, 0), True, True, False)
            batch(Batch(3, 1), True, False, False)
            store_y(Batch(3, 1), 1)
            for h in range(CHUNKS):
                sp.wait_ge(y_stored[h], 16 * BATCHES)

        @block.gpsimd
        def _(pool):
            pool.memset(identity[:, :], 0.0).then_inc(pool_setup, 1)
            pool.wait_ge(pool_setup, 1)
            pool.affine_select(out=identity[:, :], in_=identity[:, :], compare_op=ALU.not_equal, fill=1.0,
                               base=0, pattern=[[-1, 128]], channel_multiplier=1).then_inc(pool_setup, 1)
            pool.wait_ge(pool_setup, IDENTITY_MADE)
            pool.tensor_scalar(identity_r[:, :], identity[:, :], 0.0, 1.0, ALU.add, ALU.mult).then_inc(pool_setup, 1)
            made = IDENTITY_MADE + 1
            for p in range(2):
                pool.wait_ge(pool_setup, made)
                pool.memset(values[p][:, :, 2 * CHANNELS:VCOLS].bitcast(fp32), 1.0).then_inc(pool_setup, 1)
                pool.memset(values_b[p][:, :, CHANNELS:CHANNELS + 2], 1.0).then_inc(pool_setup, 1)
                pool.wait_ge(pool_setup, made + 2)
                pool.memset(q_lomax[p][HEAD:128, :].bitcast(fp32), 0.0).then_inc(pool_setup, 1)
                pool.memset(k_hione[p][HEAD:128, :].bitcast(fp32), 0.0).then_inc(pool_setup, 1)
                pool.wait_ge(pool_setup, made + 4)
                pool.memset(k_hione[p][HEAD:HEAD + 1, :].bitcast(fp32), 1.0).then_inc(pool_setup, 1)
                made += 5
            pool.wait_ge(pool_setup, made)
            pool.wait_ge(weights_loaded, 16 * WEIGHT_LOADS)
            pool.tensor_scalar(gamma_bv[:, :], b_v[:, :], gamma_col[:, :], 1.0, ALU.mult, ALU.mult).then_inc(pool_setup, 1)
            pool.wait_ge(pool_setup, SETUP_MADE)

            def add_bias(b):
                pool.wait_ge(x_loaded[b.parity], 16 * b.pair + 16)
                wait(pool, y_done, CHUNKS * (index(b) - 1))
                pool.tensor_scalar(x_bias[:, b.parity], x_sb[:, b.parity], gamma_bv[:, :], 1.0,
                                   ALU.add, ALU.mult).then_inc(x_bias_done, 1)

            def split_values(b, half):
                tiles = slice(half * CHUNK_TILES, (half + 1) * CHUNK_TILES)
                c = CHUNKS * index(b) + half
                pool.wait_ge(v_full_done, c + 1)
                wait(pool, sums_step, STEPS * (index(b) - 1))
                pool.tensor_scalar(values[b.parity][:, tiles, CHANNELS:2 * CHANNELS], v_full[:, half], 0.0, 1.0,
                                   ALU.add, ALU.mult).then_inc(v_hi_done, 1)
                pool.tensor_scalar(values_b[b.parity][:, tiles, 0:CHANNELS], v_full[:, half], 0.0, 1.0,
                                   ALU.add, ALU.mult).then_inc(values_b_done, 1)
                pool.wait_ge(v_hi_done, c + 1)
                pool.tensor_tensor(values[b.parity][:, tiles, 0:CHANNELS], v_full[:, half],
                                   values[b.parity][:, tiles, CHANNELS:2 * CHANNELS], ALU.subtract).then_inc(v_lo_done, 1)

            def low_weights(b, k):
                g, r = STEPS * index(b) + k, k % RING
                pool.wait_ge(weight_hi_done, g + 1)
                wait(pool, sums_step, g - RING + 1)
                pool.tensor_tensor(weight_lo[:, r], weight[:, r], weight_hi[:, r], ALU.subtract).then_inc(weight_lo_pool_done, 1)

            def scale(b, h):
                pool.wait_ge(sums_freed, HALVES * (CHUNKS * index(b) + h + 1))
                wait(pool, out_turned, CHUNKS * index(b) + h)
                for it in range(CHUNK_TILES):
                    last = pool.tensor_scalar(scaled[:, it], total[:, it], one_over[:, it:it + 1], gamma_col[:, :],
                                              ALU.mult, ALU.mult)
                last.then_inc(scaled_done, 1)

            def batch(b, has_prev, has_next):
                for k in range(STEPS):
                    if k + 1 in POOL_STEPS:
                        low_weights(b, k + 1)
                    if k == 4 and has_prev:
                        scale(before(b), 1)
                    if k == 6 and has_next:
                        split_values(after(b), 0)
                    if k == 7 and has_next:
                        add_bias(after(b))
                    if k == 13:
                        scale(b, 0)
                    if k == 14 and has_next:
                        split_values(after(b), 1)

            add_bias(Batch(0, 0))
            for half in range(CHUNKS):
                split_values(Batch(0, 0), half)
            for n in range(BATCHES):
                batch(Batch(n // 2, n % 2), n > 0, n < BATCHES - 1)
            scale(Batch(BATCHES // 2 - 1, 1), 1)

        @block.tensor
        def _(pe):
            pe.wait_ge(pool_setup, IDENTITY_MADE)
            pe.wait_ge(weights_loaded, 16 * WEIGHT_LOADS)
            pe.transpose(bank(0)[:, 0:128], w_qk[:, :], identity[:, :]).then_inc(w_turned, 1)
            pe.transpose(bank(1)[:, 0:128], w_v[:, :], identity[:, :]).then_inc(w_turned, 1)
            pe.wait_ge(w_ready, 2)

            def wait_read_out(bank_used, job, b):
                n = Batch(0, 0) if b is None else after(b)
                if job is None:
                    pe.wait_ge(w_ready, 2)
                elif job == "qk_next":
                    pe.wait_ge(qk_lo_done, CHUNKS * index(n) + bank_used + 1)
                elif job in ("v0_next", "v1_next"):
                    pe.wait_ge(v_full_done, CHUNKS * index(n) + int(job[1]) + 1)
                elif job.startswith("mx"):
                    pe.wait_ge(neg_max_done, mx_count(n if job.endswith("_next") else b, job))
                elif job.startswith("mt"):
                    pe.wait_ge(max_rows_done, CHUNKS * index(n if job.endswith("_next") else b) + int(job[2]) + 1)
                elif job == "out_prev":
                    pe.wait_ge(y_done, CHUNKS * index(b))
                elif job == "out_this":
                    pe.wait_ge(y_done, CHUNKS * index(b) + 1)

            def take_bank(i, job, b, flags):
                wait_read_out(i, *job_before(i, job, b, *flags))

            def project_qk(n, takes):
                pe.wait_ge(x_loaded[n.parity], 16 * n.pair + 16)
                for h in range(CHUNKS):
                    take_bank(h, "qk_next", *takes)
                    pe.matmul(bank(h), w_qk_t[:, :], x_sb[:, n.parity, chunk(h)], start=True, stop=True).then_inc(qk_done, 1)

            def project_v(n, half, takes):
                pe.wait_ge(x_loaded[n.parity], 16 * n.pair + 16)
                take_bank(0, f"v{half}_next", *takes)
                for t in range(CHUNK_TILES):
                    last = pe.matmul(bank(0)[:, tile(t)], x_sb[:, n.parity, tile(half * CHUNK_TILES + t)], w_v_t[:, :],
                                     start=True, stop=True)
                last.then_inc(v_done, 1)

            def max_scores(n, job, takes):
                p, t, h = n.parity, int(job[2]), "ab".index(job[3])
                pe.wait_ge(spread_mx[p], SPREAD_MX * n.pair + SPREAD_MX)
                take_bank(h, job, *takes)
                pe.matmul(bank(h), q_hihi[p][:, tile(t)], k_hilo[p][:, chunk(h)], start=True, stop=True).then_inc(mx_done, 1)

            def turn_max(n, h, job, takes):
                pe.wait_ge(neg_max_r_done, CHUNKS * index(n) + h + 1)
                take_bank(0, job, *takes)
                for t in range(CHUNK_TILES):
                    last = pe.transpose(bank(0)[0:1, tile(t)].bitcast(fp32r), neg_max_r[:, h * CHUNK_TILES + t:h * CHUNK_TILES + t + 1],
                                        identity_r[:, :])
                last.then_inc(mt_done, 1)

            def turn_out(n, h, job, takes):
                pe.wait_ge(scaled_done, CHUNKS * index(n) + h + 1)
                take_bank(1, job, *takes)
                for it in range(CHUNK_TILES):
                    last = pe.transpose(bank(1)[:, tile(it)], scaled[:, it], identity[:, :])
                last.then_inc(out_turned, 1)

            def do_job(job, b, n, takes):
                if job == "qk_next":
                    project_qk(n, takes)
                elif job in ("v0_next", "v1_next"):
                    project_v(n, int(job[1]), takes)
                elif job.startswith("mx"):
                    max_scores(n if job.endswith("_next") else b, job, takes)
                elif job.startswith("mt"):
                    turn_max(n if job.endswith("_next") else b, int(job[2]), job, takes)
                elif job == "out_prev":
                    turn_out(before(b), 1, job, takes)
                elif job == "out_this":
                    turn_out(b, 0, job, takes)

            def score_tile(b, k):
                h, j, p = k // TILES, k % TILES, b.parity
                if k % TILES == 0:
                    pe.wait_ge(max_rows_done, CHUNKS * index(b) + h + 1)
                if k == 0:
                    pe.wait_ge(spread_rest[p], SPREAD_REST * b.pair + SPREAD_REST)
                wait(pe, weight_hi_done, STEPS * index(b) + k - 1)
                pe.matmul(scores[:, k % 2], k_hilo[p][:, tile(j)], q_hihi[p][:, chunk(h)], start=True, stop=False)
                pe.matmul(scores[:, k % 2], k_hione[p][:, tile(j)], q_lomax[p][:, chunk(h)],
                          start=False, stop=True).then_inc(scores_done, 1)

            def weighted_sums(b, k):
                h, j, p, r = k // TILES, k % TILES, b.parity, k % RING
                g = STEPS * index(b) + k
                if j % CHUNK_TILES == 0 and h == 0:
                    half = j // CHUNK_TILES
                    pe.wait_ge(v_lo_done, CHUNKS * index(b) + half + 1)
                    pe.wait_ge(values_b_done, CHUNKS * index(b) + half + 1)
                pe.wait_ge(weight_hi_done, g + 1)

                def hi(it, stop=False):
                    return pe.matmul(sums[:, it, 0:VCOLS], weight_hi[:, r, tile(it)], values[p][:, j],
                                     start=(j == 0), stop=stop)

                def lo(it):
                    return pe.matmul(sums[:, it, CHANNELS:VCOLS], weight_lo[:, r, tile(it)], values_b[p][:, j],
                                     start=False, stop=False)

                if j < TILES - 1:
                    for it in range(CHUNK_TILES):
                        if j == 0 and it % HALF_TILES == 0:
                            wait(pe, sums_freed, HALVES * (CHUNKS * index(b) + h - 1) + it // HALF_TILES + 1)
                        hi(it)
                    pe.wait_ge(weight_lo_pool_done if k in POOL_STEPS else weight_lo_done, lo_count(b, k))
                    for it in range(CHUNK_TILES):
                        last = lo(it)
                    last.then_inc(sums_step, 1)
                else:
                    pe.wait_ge(weight_lo_pool_done if k in POOL_STEPS else weight_lo_done, lo_count(b, k))
                    for it in range(CHUNK_TILES):
                        last = lo(it)
                    last.then_inc(sums_step, 1)
                    for it in range(CHUNK_TILES):
                        last = hi(it, stop=True)
                        if it % HALF_TILES == HALF_TILES - 1:
                            last.then_inc(sums_done, 1)

            for job in PROLOGUE_JOBS:
                if job == "mt0_next":
                    pe.wait_ge(pool_setup, SETUP_MADE)
                do_job(job, None, Batch(0, 0), (None, (False, False)))
            for k in range(AHEAD):
                score_tile(Batch(0, 0), k)

            def batch(b, has_prev, has_next):
                for k in range(STEPS):
                    if k + AHEAD < STEPS:
                        score_tile(b, k + AHEAD)
                    elif has_next:
                        score_tile(after(b), k + AHEAD - STEPS)
                    ahead, behind = jobs_of(k, has_prev, has_next)
                    for job in ahead:
                        do_job(job, b, after(b), (b, (has_prev, has_next)))
                    weighted_sums(b, k)
                    for job in behind:
                        do_job(job, b, after(b), (b, (has_prev, has_next)))

            over_batches(pe, batch)
            last_batch = Batch(BATCHES // 2 - 1, 1)
            pe.wait_ge(scaled_done, CHUNKS * BATCHES)
            wait_read_out(1, "out_this", last_batch)
            for it in range(CHUNK_TILES):
                last = pe.transpose(bank(1)[:, tile(it)], scaled[:, it], identity[:, :])
            last.then_inc(out_turned, 1)

        @block.scalar
        def _(act):
            act.dma_start(w_qk[0:HEAD, :], Wq).then_inc(weights_loaded, 16)
            act.dma_start(w_qk[HEAD:2 * HEAD, :], Wk).then_inc(weights_loaded, 16)
            act.dma_start(w_v[:, :], Wv).then_inc(weights_loaded, 16)
            act.wait_ge(weights_loaded, 16 * WEIGHT_LOADS)

            def round_qk(n):
                for h in range(CHUNKS):
                    act.wait_ge(qk_done, CHUNKS * index(n) + h + 1)
                    if h == 0:
                        m = before(n)
                        if not isinstance(index(n), int) or index(n) > 0:
                            act.wait_ge(spread_rest[m.parity], SPREAD_REST * m.pair + SPREAD_REST)
                            act.wait_ge(spread_mx[m.parity], SPREAD_MX * m.pair + SPREAD_MX)
                    act.activation(qk_hi[:, chunk(h)], bank(h), ACT.Identity, bias=b_qk[:, :]).then_inc(qk_hi_done, 1)

            def take_v(n, half):
                c = CHUNKS * index(n) + half
                act.wait_ge(v_done, c + 1)
                wait(act, v_lo_done, c - 1)
                act.activation(v_full[:, half], bank(0).rearrange("p (t c) -> p t c", c=CHANNELS),
                               ACT.Copy).then_inc(v_full_done, 1)

            def write_max_rows(n, h):
                act.wait_ge(mt_done, CHUNKS * index(n) + h + 1)
                done = act.activation(q_lomax[n.parity][HEAD:HEAD + 1, chunk(h)], bank(0)[0:1, :], ACT.Copy)
                done.then_inc(max_rows_done, 1)

            def do_job(job, b, n):
                if job == "qk_next":
                    round_qk(n)
                elif job in ("v0_next", "v1_next"):
                    take_v(n, int(job[1]))
                elif job.startswith("mt"):
                    write_max_rows(n if job.endswith("_next") else b, int(job[2]))

            def wait_low(b, k):
                act.wait_ge(weight_lo_pool_done if k in POOL_STEPS else weight_lo_done, lo_count(b, k))

            def exponentials(b, k):
                g, r = STEPS * index(b) + k, k % RING
                act.wait_ge(scores_done, g + 1)
                if k >= RING:
                    wait_low(b, k - RING)
                elif not isinstance(index(b), int) or index(b) > 0:
                    wait_low(before(b), k - RING + STEPS)
                act.activation(weight[:, r], scores[:, k % 2], ACT.Exp)
                wait(act, sums_step, g - RING + 1)
                act.activation(weight_hi[:, r], scores[:, k % 2], ACT.Exp).then_inc(weight_hi_done, 1)

            def take_low_sum(b, h):
                for half in range(HALVES):
                    c = HALVES * (CHUNKS * index(b) + h) + half
                    its = slice(half * HALF_TILES, (half + 1) * HALF_TILES)
                    act.wait_ge(sums_done, c + 1)
                    wait(act, sums_freed, c - HALVES + 1)
                    act.activation(low_sum[:, its], sums[:, its, 0:CHANNELS], ACT.Copy).then_inc(low_sum_done, 1)

            for job in PROLOGUE_JOBS:
                if job == "mt0_next":
                    act.wait_ge(pool_setup, SETUP_MADE)
                do_job(job, None, Batch(0, 0))
            for k in range(AHEAD):
                exponentials(Batch(0, 0), k)

            def batch(b, has_prev, has_next):
                for k in range(STEPS):
                    if k == 0 and has_prev:
                        take_low_sum(before(b), 1)
                    if k == TILES:
                        take_low_sum(b, 0)
                    if k + AHEAD < STEPS:
                        exponentials(b, k + AHEAD)
                    elif has_next:
                        exponentials(after(b), k + AHEAD - STEPS)
                    for job in sum(jobs_of(k, has_prev, has_next), []):
                        do_job(job, b, after(b))

            over_batches(act, batch)
            take_low_sum(Batch(BATCHES // 2 - 1, 1), 1)

        @block.vector
        def _(dve):
            for i, w in enumerate((w_qk_t, w_v_t)):
                dve.wait_ge(w_turned, i + 1)
                done = dve.tensor_copy(w[:, :], bank(i)[:, 0:128])
                done.then_inc(w_ready, 1)
            dve.wait_ge(weights_loaded, 16 * WEIGHT_LOADS)

            def rest_of_qk(n):
                for h in range(CHUNKS):
                    dve.wait_ge(qk_hi_done, CHUNKS * index(n) + h + 1)
                    done = dve.scalar_tensor_tensor(qk_lo[:, chunk(h)], bank(h), b_qk[:, :], qk_hi[:, chunk(h)],
                                                    ALU.add, ALU.subtract)
                    done.then_inc(qk_lo_done, 1)

            def maximum(n, job):
                t, h = int(job[2]), "ab".index(job[3])
                dve.wait_ge(mx_done, mx_count(n, job))
                dve.reduce_max(neg_max[:, h, t:t + 1], bank(h), AX.X, negate=True).then_inc(neg_max_done, 1)
                if t % CHUNK_TILES == CHUNK_TILES - 1 and h == 1:
                    c = CHUNKS * index(n) + t // CHUNK_TILES
                    cols = slice(t + 1 - CHUNK_TILES, t + 1)
                    dve.wait_ge(neg_max_done, mx_count(n, job))
                    wait(dve, mt_done, c - 1)
                    dve.tensor_tensor(neg_max_r[:, cols], neg_max[:, 0, cols], neg_max[:, 1, cols],
                                      ALU.min).then_inc(neg_max_r_done, 1)

            def finish(n, h):
                c = CHUNKS * index(n) + h
                dve.wait_ge(out_turned, c + 1)
                dve.wait_ge(x_bias_done, index(n) + 1)
                wait(dve, y_stored[h], 16 * index(n))
                done = dve.tensor_tensor(y_sb[:, h], bank(1), x_bias[:, n.parity, chunk(h)], ALU.add)
                done.then_inc(y_done, 1)

            def do_job(job, b, n):
                if job == "qk_next":
                    rest_of_qk(n)
                elif job.startswith("mx"):
                    maximum(n if job.endswith("_next") else b, job)
                elif job == "out_prev":
                    finish(before(b), 1)
                elif job == "out_this":
                    finish(b, 0)

            def low_weights(b, k):
                g, r = STEPS * index(b) + k, k % RING
                dve.wait_ge(weight_hi_done, g + 1)
                wait(dve, sums_step, g - RING + 1)
                dve.tensor_tensor(weight_lo[:, r], weight[:, r], weight_hi[:, r], ALU.subtract).then_inc(weight_lo_done, 1)

            def add_sums(b, h):
                for half in range(HALVES):
                    c = HALVES * (CHUNKS * index(b) + h) + half
                    its = slice(half * HALF_TILES, (half + 1) * HALF_TILES)
                    dve.wait_ge(low_sum_done, c + 1)
                    if half == 0:
                        wait(dve, scaled_done, CHUNKS * index(b) + h)
                    dve.reciprocal(one_over[:, its], sums[:, its, 2 * CHANNELS])
                    dve.tensor_tensor(total[:, its], sums[:, its, CHANNELS:2 * CHANNELS], low_sum[:, its],
                                      ALU.add).then_inc(sums_freed, 1)

            for job in PROLOGUE_JOBS:
                do_job(job, None, Batch(0, 0))
            low_weights(Batch(0, 0), 0)

            def batch(b, has_prev, has_next):
                for k in range(STEPS):
                    if k == 0 and has_prev:
                        add_sums(before(b), 1)
                    if k == TILES:
                        add_sums(b, 0)
                    if k + 1 < STEPS:
                        if k + 1 not in POOL_STEPS:
                            low_weights(b, k + 1)
                    elif has_next:
                        low_weights(after(b), 0)
                    for job in sum(jobs_of(k, has_prev, has_next), []):
                        do_job(job, b, after(b))

            over_batches(dve, batch)
            last_batch = Batch(BATCHES // 2 - 1, 1)
            add_sums(last_batch, 1)
            finish(last_batch, 1)


_INS = ["x", "L0_conv_Wq", "L0_conv_bq", "L0_conv_Wk", "L0_conv_bk", "L0_conv_Wv", "L0_conv_bv", "L0_conv_gamma"]
_OUT = (BATCHES, CHANNELS, 32, 32)


def kernel(**inputs):
    import numpy as np
    import concourse.bacc as bacc
    from concourse.bass_utils import run_bass_kernel_spmd

    nc = bacc.Bacc("TRN2", target_bir_lowering=False, num_devices=1)
    arrays, args = {}, []
    for name in _INS:
        a = np.ascontiguousarray(inputs[name])
        arrays[f"in_{name}"] = a
        args.append(nc.dram_tensor(f"in_{name}", a.shape, mybir.dt.from_np(a.dtype), kind="ExternalInput").ap())
    args.append(nc.dram_tensor("out_0", _OUT, mybir.dt.float32, kind="ExternalOutput").ap())
    attention_program(nc, *args)
    result = run_bass_kernel_spmd(nc, [arrays], core_ids=[0])
    return result.results[0]["out_0"]
```

```python
from collections import namedtuple
from contextlib import ExitStack

import concourse.bass as bass
import concourse.mybir as mybir

BATCHES = 8
CHANNELS = 128
HEAD = 64
PIXELS = 32 * 32
TILE = 128
CHUNK = 512
CHUNKS = PIXELS // CHUNK
TILES = PIXELS // TILE
CHUNK_TILES = CHUNK // TILE
STEPS = CHUNKS * TILES
AHEAD = 2
HALVES = 2
HALF_TILES = CHUNK_TILES // HALVES
RING = 4
VCOLS = 2 * CHANNELS + 2
IDENTITY_MADE = 2
SETUP_MADE = 15
WARM_UP = (14, 4)

JOBS = {
    0: ([], ["mx4a", "mx4b"], []),
    1: ([], ["mx5a"], ["mx5b"]),
    2: ([], ["mx6a"], []),
    3: (["mx6b"], ["mx7a"], []),
    4: (["qk0_next", "mx7b"], [], []),
    5: ([], ["qk1_next"], ["mt1"]),
    6: ([], [], []),
    7: ([], [], []),
    8: (["v0_next"], ["out_prev"], []),
    9: ([], ["mx0a_next", "mx0b_next"], ["mx1a_next"]),
    10: ([], ["mx1b_next"], []),
    11: ([], ["mx2a_next", "mx2b_next"], []),
    12: (["mx3a_next"], ["mx3b_next"], ["v1_next"]),
    13: (["mt0_next"], [], []),
    14: ([], [], []),
    15: ([], ["out_this"], []),
}
EARLY = ("qk0_next", "v0_next", "mt0_next")
DVE_EARLY = ("mx4a", "mx4b", "mx5a", "mx5b", "mx6a", "mx7b", "out_prev", "mx1b_next", "mx3a_next", "mx3b_next")
SCALE_PREV, SCALE_THIS, SPLIT, ADD_BIAS = 7, 14, (10, 15), 8
X_HI, X_LO = (0, 2), (0, 3)
FIRST = ["k0", "q0", "k1", "q1"]
FIRST_LO = ["k0", "k1", "q0", "q1"]
POOL_STEPS = (1, 2, 3, 4, 5, 10, 11, 12)
SPREAD_MX, SPREAD_REST = 4, 2

BANKS = {"qk0_next": 0, "qk1_next": 1, "v0_next": 0, "v1_next": 0, "mt0_next": 1, "mt1": 0,
         "out_prev": 1, "out_this": 1}


def bank_of(job):
    return "ab".index(job[3]) if job.startswith("mx") else BANKS[job]


def bank_order(bank, jobs):
    return [j for j in jobs if bank_of(j) == bank]


Batch = namedtuple("Batch", "pair parity")
LAST = Batch(BATCHES // 2 - 1, 1)


def index(b):
    return 2 * b.pair + b.parity


def after(b):
    return Batch(b.pair, 1) if b.parity == 0 else Batch(b.pair + 1, 0)


def before(b):
    return Batch(b.pair, 0) if b.parity == 1 else Batch(b.pair - 1, 1)


def over_batches(engine, batch_body):
    batch_body(Batch(0, 0), False, True)
    with engine.Fori(0, BATCHES // 2 - 1) as pair:
        batch_body(Batch(pair, 1), True, True)
        batch_body(Batch(pair + 1, 0), True, True)
    batch_body(LAST, True, False)


def lo_count(b, k):
    mine = [i for i in range(STEPS) if (i in POOL_STEPS) == (k in POOL_STEPS)]
    return len(mine) * index(b) + mine.index(k) + 1


def mx_count(b, job):
    return 2 * TILES * index(b) + 2 * int(job[2]) + "ab".index(job[3]) + 1


def jobs_of(step, has_prev, has_next):
    return [[j for j in jobs if (has_prev or j != "out_prev")
             and (has_next or not (j.endswith("_next") or j == "out_this"))]
            for jobs in JOBS[step]]


def all_jobs(has_prev, has_next):
    return [j for step in range(STEPS) for jobs in jobs_of(step, has_prev, has_next) for j in jobs]


def wait(engine, semaphore, count):
    if isinstance(count, int) and count <= 0:
        return
    engine.wait_ge(semaphore, count)


def job_before(bank, job, b, has_prev, has_next):
    order = bank_order(bank, all_jobs(has_prev, has_next))
    i = order.index(job)
    if i:
        return order[i - 1], b
    if not has_prev:
        return None, None
    return bank_order(bank, all_jobs(True, True))[-1], before(b)


def loads(b, each=1):
    return 16 * each * (b.pair + b.parity)


def qk_count(b, h):
    return CHUNKS * (index(b) - 1) + h + 1


def attention_program(nc, x, Wq, bq, Wk, bk, Wv, bv, gamma, out):
    fp32 = mybir.dt.float32
    fp32r = mybir.dt.float32r
    bf16 = mybir.dt.bfloat16
    ALU = mybir.AluOpType
    ACT = mybir.ActivationFunctionType
    AX = mybir.AxisListType

    x_dram = x.rearrange("b c h w -> b c (h w)")
    out_dram = out.rearrange("b c h w -> b c (h w)")

    with ExitStack() as ctx:
        def sbuf(name, shape, dtype):
            return ctx.enter_context(nc.sbuf_tensor(name, shape, dtype))

        def psum(name, shape, dtype):
            return ctx.enter_context(nc.psum_tensor(name, shape, dtype))

        def sem(name):
            return ctx.enter_context(nc.semaphore(name))

        identity = sbuf("identity", [128, 128], fp32)
        identity_r = sbuf("identity_r", [128, 128], fp32r)
        w_qk = sbuf("w_qk", [2 * HEAD, CHANNELS], fp32)
        w_v = sbuf("w_v", [CHANNELS, CHANNELS], fp32)
        w_qk_t = sbuf("w_qk_t", [CHANNELS, 2 * HEAD], fp32)
        w_qk_hi = sbuf("w_qk_hi", [CHANNELS, 2 * HEAD], fp32r)
        w_qk_lo = sbuf("w_qk_lo", [CHANNELS, 2 * HEAD], fp32r)
        w_v_t = sbuf("w_v_t", [CHANNELS, CHANNELS], fp32)
        w_kk_t = sbuf("w_kk_t", [CHANNELS, 2, HEAD], fp32)
        w_qq_t = sbuf("w_qq_t", [CHANNELS, 2, HEAD], fp32)
        b_qk = sbuf("b_qk", [2 * HEAD, 1], fp32)
        b_kk = sbuf("b_kk", [2 * HEAD, 1], fp32)
        b_qq = sbuf("b_qq", [2 * HEAD, 1], fp32)
        exp_of_identity = sbuf("exp_of_identity", [128, 1], fp32)
        b_v = sbuf("b_v", [CHANNELS, 1], fp32)
        gamma_col = sbuf("gamma_col", [128, 1], fp32)
        gamma_bv = sbuf("gamma_bv", [128, 1], fp32)
        x_sb = sbuf("x_sb", [CHANNELS, 2, PIXELS], fp32)
        x_bias = sbuf("x_bias", [CHANNELS, 2, PIXELS], fp32)
        x_hi = sbuf("x_hi", [CHANNELS, PIXELS], fp32r)
        x_lo = sbuf("x_lo", [CHANNELS, PIXELS], fp32r)
        v_full = sbuf("v_full", [TILE, 2, CHUNK_TILES, CHANNELS], fp32)
        qk_hi = sbuf("qk_hi", [2 * HEAD, PIXELS], fp32r)
        qk_lo = sbuf("qk_lo", [2 * HEAD, PIXELS], fp32r)
        q_hihi = [sbuf(f"q_hihi{p}", [128, PIXELS], fp32r) for p in range(2)]
        k_hilo = [sbuf(f"k_hilo{p}", [128, PIXELS], fp32r) for p in range(2)]
        q_lomax = [sbuf(f"q_lomax{p}", [128, PIXELS], fp32r) for p in range(2)]
        k_hione = [sbuf(f"k_hione{p}", [128, PIXELS], fp32r) for p in range(2)]
        values = [sbuf(f"values{p}", [TILE, TILES, VCOLS], fp32r) for p in range(2)]
        values_b = [sbuf(f"values_b{p}", [TILE, TILES, CHANNELS + 2], bf16) for p in range(2)]
        neg_max = sbuf("neg_max", [TILE, 2, TILES], fp32)
        neg_max_r = sbuf("neg_max_r", [TILE, TILES], fp32r)
        weight = sbuf("weight", [TILE, RING, CHUNK], fp32)
        weight_hi = sbuf("weight_hi", [TILE, RING, CHUNK], fp32r)
        weight_lo = sbuf("weight_lo", [TILE, RING, CHUNK], bf16)
        low_sum = sbuf("low_sum", [TILE, CHUNK_TILES, CHANNELS + 1], fp32)
        total = sbuf("total", [TILE, CHUNK_TILES, CHANNELS + 1], fp32)
        one_over = sbuf("one_over", [TILE, CHUNK_TILES], fp32)
        scaled = sbuf("scaled", [TILE, CHUNK_TILES, CHANNELS], fp32)
        y_sb = sbuf("y_sb", [CHANNELS, CHUNKS, CHUNK], fp32)

        scores = psum("scores", [TILE, 2, CHUNK], fp32)
        sums = psum("sums", [TILE, CHUNK_TILES, CHUNK], fp32)
        work = psum("work", [128, 2 * CHUNK], fp32)

        w_qk_loaded = sem("w_qk_loaded")
        biases_loaded = sem("biases_loaded")
        rest_loaded = sem("rest_loaded")
        first_x_loaded = [sem(f"first_x_loaded{h}") for h in range(CHUNKS)]
        x_loaded = [sem(f"x_loaded{p}") for p in range(2)]
        spread_mx = [sem(f"spread_mx{p}") for p in range(2)]
        spread_rest = [sem(f"spread_rest{p}") for p in range(2)]
        last_stored = sem("last_stored")
        y_stored = [sem(f"y_stored{h}") for h in range(CHUNKS)]
        pool_setup = sem("pool_setup")
        x_lo_done = sem("x_lo_done")
        x_bias_done = sem("x_bias_done")
        v_hi_done = sem("v_hi_done")
        v_lo_done = sem("v_lo_done")
        values_b_done = sem("values_b_done")
        weight_lo_pool_done = sem("weight_lo_pool_done")
        scaled_done = sem("scaled_done")
        w_turned = sem("w_turned")
        first_done = sem("first_done")
        qk_done = sem("qk_done")
        v_done = sem("v_done")
        mx_done = sem("mx_done")
        mt_done = sem("mt_done")
        scores_done = sem("scores_done")
        sums_step = sem("sums_step")
        sums_done = sem("sums_done")
        out_turned = sem("out_turned")
        first_hi_done = sem("first_hi_done")
        first_ones_done = sem("first_ones_done")
        w_v_ready = sem("w_v_ready")
        x_hi_done = sem("x_hi_done")
        qk_hi_done = sem("qk_hi_done")
        v_full_done = sem("v_full_done")
        weight_hi_done = sem("weight_hi_done")
        low_sum_done = sem("low_sum_done")
        max_rows_done = sem("max_rows_done")
        w_ready = sem("w_ready")
        b_ready = sem("b_ready")
        first_lo_done = sem("first_lo_done")
        qk_lo_done = sem("qk_lo_done")
        neg_max_done = sem("neg_max_done")
        neg_max_r_done = sem("neg_max_r_done")
        weight_lo_done = sem("weight_lo_done")
        sums_freed = sem("sums_freed")
        one_over_done = sem("one_over_done")
        y_done = sem("y_done")
        last_scaled = sem("last_scaled")

        block = ctx.enter_context(nc.Block())

        def bank(i):
            return work[:, i * CHUNK:(i + 1) * CHUNK]

        def chunk(h):
            return slice(h * CHUNK, (h + 1) * CHUNK)

        def tile(t):
            return slice(t * TILE, (t + 1) * TILE)

        def tiles_of_half(half):
            return range(half * HALF_TILES, (half + 1) * HALF_TILES)

        def half_columns(half):
            return slice(half * HALF_TILES * TILE, (half + 1) * HALF_TILES * TILE)

        def wait_x(engine, b):
            if not isinstance(index(b), int) or index(b) > 0:
                engine.wait_ge(x_loaded[b.parity], loads(b))
            else:
                for h in range(CHUNKS):
                    engine.wait_ge(first_x_loaded[h], 16)

        @block.sync
        def _(sp):
            def image(dram, b):
                n = index(b)
                return dram[n] if isinstance(n, int) else dram[bass.ds(sp.snap(n), 1)].rearrange("b c n -> (b c) n")

            def x_of(b):
                return image(x_dram, b)

            def load_x(b, source):
                sp.dma_start(x_sb[:, b.parity], source).then_inc(x_loaded[b.parity], 16)

            def spread(b):
                p = b.parity
                sp.wait_ge(qk_hi_done, qk_count(b, CHUNKS - 1))
                sp.dma_start(k_hilo[p][0:HEAD, :].bitcast(fp32), qk_hi[HEAD:2 * HEAD, :].bitcast(fp32)).then_inc(spread_mx[p], 16)
                sp.dma_start(q_hihi[p][0:HEAD, :].bitcast(fp32), qk_hi[0:HEAD, :].bitcast(fp32)).then_inc(spread_mx[p], 16)
                sp.dma_start(q_hihi[p][HEAD:2 * HEAD, :].bitcast(fp32), qk_hi[0:HEAD, :].bitcast(fp32)).then_inc(spread_mx[p], 16)
                sp.wait_ge(qk_lo_done, qk_count(b, CHUNKS - 1))
                sp.dma_start(k_hilo[p][HEAD:2 * HEAD, :].bitcast(fp32), qk_lo[HEAD:2 * HEAD, :].bitcast(fp32)).then_inc(spread_mx[p], 16)
                sp.dma_start(q_lomax[p][0:HEAD, :].bitcast(fp32), qk_lo[0:HEAD, :].bitcast(fp32)).then_inc(spread_rest[p], 16)
                sp.dma_start(k_hione[p][0:HEAD, :].bitcast(fp32), qk_hi[HEAD:2 * HEAD, :].bitcast(fp32)).then_inc(spread_rest[p], 16)

            def store_y(b, h):
                place = image(out_dram, b)
                sp.wait_ge(y_done, CHUNKS * index(b) + h + 1)
                sp.dma_start(place[:, chunk(h)], y_sb[:, h]).then_inc(y_stored[h], 16)

            def batch(b, has_prev, has_next, load):
                if load:
                    source = x_of(after(after(b)))
                    sp.wait_ge(v_lo_done, CHUNKS * index(b) + CHUNKS)
                    load_x(after(after(b)), source)
                if has_next:
                    spread(after(b))
                if has_prev:
                    store_y(before(b), 1)
                store_y(b, 0)

            sp.dma_start(w_qk[HEAD:2 * HEAD, :], Wk).then_inc(w_qk_loaded, 16)
            sp.dma_start(x_sb[:, 0, chunk(0)], x_dram[0][:, chunk(0)]).then_inc(first_x_loaded[0], 16)
            for half in range(2):
                sp.dma_start(b_qq[half * HEAD:(half + 1) * HEAD, :],
                             bq.rearrange("(p a) -> p a", a=1)).then_inc(biases_loaded, 16)
            sp.dma_start(x_sb[:, 0, chunk(1)], x_dram[0][:, chunk(1)]).then_inc(first_x_loaded[1], 16)
            sp.dma_start(w_v[:, :], Wv).then_inc(rest_loaded, 16)
            sp.dma_start(b_v[:, :], bv.rearrange("(p a) -> p a", a=1)).then_inc(rest_loaded, 16)
            sp.dma_start(gamma_col[:, :], gamma.rearrange("(p a) -> p a", a=1).broadcast_to([128, 1])).then_inc(rest_loaded, 16)
            load_x(Batch(0, 1), x_of(Batch(0, 1)))
            batch(Batch(0, 0), False, True, True)
            with sp.Fori(0, BATCHES // 2 - 2) as pair:
                batch(Batch(pair, 1), True, True, True)
                batch(Batch(pair + 1, 0), True, True, True)
            batch(Batch(2, 1), True, True, True)
            batch(Batch(3, 0), True, True, False)
            batch(LAST, True, False, False)
            for half in range(HALVES):
                cols = half_columns(half)
                sp.wait_ge(y_done, CHUNKS * BATCHES + half)
                sp.dma_start(out_dram[BATCHES - 1][:, chunk(1)][:, cols], y_sb[:, 1, cols]).then_inc(last_stored, 16)
            sp.wait_ge(y_stored[0], 16 * BATCHES)
            sp.wait_ge(y_stored[1], 16 * (BATCHES - 1))
            sp.wait_ge(last_stored, 16 * HALVES)

        @block.gpsimd
        def _(pool):
            pool.memset(identity[:, :], 0.0).then_inc(pool_setup, 1)
            pool.wait_ge(pool_setup, 1)
            pool.affine_select(out=identity[:, :], in_=identity[:, :], compare_op=ALU.not_equal, fill=1.0,
                               base=0, pattern=[[-1, 128]], channel_multiplier=1).then_inc(pool_setup, 1)
            pool.wait_ge(pool_setup, IDENTITY_MADE)
            pool.tensor_scalar(identity_r[:, :], identity[:, :], 0.0, 1.0, ALU.add, ALU.mult).then_inc(pool_setup, 1)
            pool.memset(low_sum[:, :, CHANNELS:CHANNELS + 1], 0.0).then_inc(pool_setup, 1)
            made = IDENTITY_MADE + 2
            for p in range(2):
                pool.wait_ge(pool_setup, made)
                pool.memset(values[p][:, :, 2 * CHANNELS:VCOLS].bitcast(fp32), 1.0).then_inc(pool_setup, 1)
                pool.memset(values_b[p][:, :, CHANNELS:CHANNELS + 2], 1.0).then_inc(pool_setup, 1)
                pool.wait_ge(pool_setup, made + 2)
                pool.memset(q_lomax[p][HEAD:128, :].bitcast(fp32), 0.0).then_inc(pool_setup, 1)
                pool.memset(k_hione[p][HEAD:128, :].bitcast(fp32), 0.0).then_inc(pool_setup, 1)
                pool.wait_ge(pool_setup, made + 4)
                pool.memset(k_hione[p][HEAD:HEAD + 1, :].bitcast(fp32), 1.0).then_inc(pool_setup, 1)
                made += 5
            pool.wait_ge(pool_setup, made)
            pool.wait_ge(rest_loaded, 3 * 16)
            pool.tensor_scalar(gamma_bv[:, :], b_v[:, :], gamma_col[:, :], 1.0, ALU.mult, ALU.mult).then_inc(pool_setup, 1)
            pool.wait_ge(pool_setup, SETUP_MADE)

            def add_bias(b):
                wait_x(pool, b)
                wait(pool, y_done, CHUNKS * (index(b) - 1))
                pool.tensor_scalar(x_bias[:, b.parity], x_sb[:, b.parity], gamma_bv[:, :], 1.0,
                                   ALU.add, ALU.mult).then_inc(x_bias_done, 1)

            def split_values(b, half):
                tiles = slice(half * CHUNK_TILES, (half + 1) * CHUNK_TILES)
                c = CHUNKS * index(b) + half
                pool.wait_ge(v_full_done, c + 1)
                wait(pool, sums_step, STEPS * (index(b) - 1))
                pool.tensor_scalar(values[b.parity][:, tiles, CHANNELS:2 * CHANNELS], v_full[:, half], 0.0, 1.0,
                                   ALU.add, ALU.mult).then_inc(v_hi_done, 1)
                pool.tensor_scalar(values_b[b.parity][:, tiles, 0:CHANNELS], v_full[:, half], 0.0, 1.0,
                                   ALU.add, ALU.mult).then_inc(values_b_done, 1)
                pool.wait_ge(v_hi_done, c + 1)
                pool.tensor_tensor(values[b.parity][:, tiles, 0:CHANNELS], v_full[:, half],
                                   values[b.parity][:, tiles, CHANNELS:2 * CHANNELS], ALU.subtract).then_inc(v_lo_done, 1)

            def low_weights(b, k):
                g, r = STEPS * index(b) + k, k % RING
                pool.wait_ge(weight_hi_done, g + 1)
                wait(pool, sums_step, g - RING + 1)
                pool.tensor_tensor(weight_lo[:, r], weight[:, r], weight_hi[:, r], ALU.subtract).then_inc(weight_lo_pool_done, 1)

            def scale(b, h):
                pool.wait_ge(one_over_done, CHUNKS * index(b) + h + 1)
                wait(pool, out_turned, CHUNKS * index(b) + h)
                for it in range(CHUNK_TILES):
                    last = pool.tensor_scalar(scaled[:, it], total[:, it, 0:CHANNELS], one_over[:, it:it + 1], gamma_col[:, :],
                                              ALU.mult, ALU.mult)
                last.then_inc(scaled_done, 1)

            def batch(b, has_prev, has_next):
                for k in range(STEPS):
                    if k + 1 in POOL_STEPS:
                        low_weights(b, k + 1)
                    if k + 1 == STEPS and 0 in POOL_STEPS and has_next:
                        low_weights(after(b), 0)
                    if k == SCALE_PREV and has_prev:
                        scale(before(b), 1)
                    if k == ADD_BIAS and has_next:
                        add_bias(after(b))
                    if k in SPLIT and has_next:
                        split_values(after(b), SPLIT.index(k))
                    if k == SCALE_THIS:
                        scale(b, 0)

            pool.wait_ge(w_ready, 3)
            pool.tensor_scalar(w_qk_hi[:, :], w_qk_t[:, :], 0.0, 1.0, ALU.add, ALU.mult).then_inc(pool_setup, 1)
            pool.wait_ge(pool_setup, SETUP_MADE + 1)
            pool.tensor_tensor(w_qk_lo[:, :], w_qk_t[:, :], w_qk_hi[:, :], ALU.subtract).then_inc(pool_setup, 1)
            add_bias(Batch(0, 0))
            for half in range(CHUNKS):
                split_values(Batch(0, 0), half)
            for n in range(BATCHES):
                batch(Batch(n // 2, n % 2), n > 0, n < BATCHES - 1)

        @block.tensor
        def _(pe):
            def wait_read_out(bank_used, job, b):
                n = Batch(0, 0) if b is None else after(b)
                if job is None:
                    pe.wait_ge(first_lo_done, FIRST_LO.index(f"q{bank_used}") + 1)
                elif job in ("qk0_next", "qk1_next"):
                    pe.wait_ge(qk_lo_done, qk_count(n, int(job[2])))
                elif job in ("v0_next", "v1_next"):
                    pe.wait_ge(v_full_done, CHUNKS * index(n) + int(job[1]) + 1)
                elif job.startswith("mx"):
                    pe.wait_ge(neg_max_done, mx_count(n if job.endswith("_next") else b, job))
                elif job.startswith("mt"):
                    pe.wait_ge(max_rows_done, CHUNKS * index(n if job.endswith("_next") else b) + int(job[2]) + 1)
                elif job == "out_prev":
                    pe.wait_ge(y_done, CHUNKS * index(b))
                elif job == "out_this":
                    pe.wait_ge(y_done, CHUNKS * index(b) + 1)

            def take_bank(job, b, flags):
                wait_read_out(bank_of(job), *job_before(bank_of(job), job, b, *flags))
                return bank(bank_of(job))

            def project_qk(n, h, place):
                pe.matmul(place, w_qk_hi[:, :], x_hi[:, chunk(h)], start=True, stop=False)
                pe.matmul(place, w_qk_lo[:, :], x_hi[:, chunk(h)], start=False, stop=False)
                pe.matmul(place, w_qk_hi[:, :], x_lo[:, chunk(h)], start=False, stop=True).then_inc(qk_done, 1)

            def project_v(n, half, place):
                for t in range(CHUNK_TILES):
                    last = pe.matmul(place[:, tile(t)], x_sb[:, n.parity, tile(half * CHUNK_TILES + t)], w_v_t[:, :],
                                     start=True, stop=True)
                last.then_inc(v_done, 1)

            def max_scores(n, t, h, place):
                p = n.parity
                pe.matmul(place, q_hihi[p][:, tile(t)], k_hilo[p][:, chunk(h)], start=True, stop=True).then_inc(mx_done, 1)

            def turn_max(h, place):
                for t in range(CHUNK_TILES):
                    last = pe.transpose(place[0:1, tile(t)].bitcast(fp32r), neg_max_r[:, h * CHUNK_TILES + t:h * CHUNK_TILES + t + 1],
                                        identity_r[:, :])
                last.then_inc(mt_done, 1)

            def turn_out(its, place):
                for it in its:
                    last = pe.transpose(place[:, tile(it)], scaled[:, it], identity[:, :])
                last.then_inc(out_turned, 1)

            def do_job(job, b, n, takes):
                if job in ("qk0_next", "qk1_next"):
                    pe.wait_ge(x_lo_done, qk_count(n, int(job[2])))
                    project_qk(n, int(job[2]), take_bank(job, *takes))
                elif job in ("v0_next", "v1_next"):
                    wait_x(pe, n)
                    project_v(n, int(job[1]), take_bank(job, *takes))
                elif job.startswith("mx"):
                    if job.endswith("_next"):
                        pe.wait_ge(spread_mx[n.parity], loads(n, SPREAD_MX))
                    max_scores(n if job.endswith("_next") else b, int(job[2]), "ab".index(job[3]), take_bank(job, *takes))
                elif job.startswith("mt"):
                    m, h = n if job.endswith("_next") else b, int(job[2])
                    pe.wait_ge(neg_max_r_done, CHUNKS * index(m) + h + 1)
                    turn_max(h, take_bank(job, *takes))
                elif job in ("out_prev", "out_this"):
                    m, h = (before(b), 1) if job == "out_prev" else (b, 0)
                    pe.wait_ge(scaled_done, CHUNKS * index(m) + h + 1)
                    turn_out(range(CHUNK_TILES), take_bank(job, *takes))

            def score_tile(b, k):
                h, j, p = k // TILES, k % TILES, b.parity
                if k % TILES == 0:
                    pe.wait_ge(max_rows_done, CHUNKS * index(b) + h + 1)
                if k == 0 and (not isinstance(index(b), int) or index(b) > 0):
                    pe.wait_ge(spread_rest[p], loads(b, SPREAD_REST))
                wait(pe, weight_hi_done, STEPS * index(b) + k - 1)
                pe.matmul(scores[:, k % 2], k_hilo[p][:, tile(j)], q_hihi[p][:, chunk(h)], start=True, stop=False)
                pe.matmul(scores[:, k % 2], k_hione[p][:, tile(j)], q_lomax[p][:, chunk(h)],
                          start=False, stop=True).then_inc(scores_done, 1)

            def weighted_sums(b, k):
                h, j, p, r = k // TILES, k % TILES, b.parity, k % RING
                g = STEPS * index(b) + k
                if j % CHUNK_TILES == 0 and h == 0:
                    half = j // CHUNK_TILES
                    pe.wait_ge(v_lo_done, CHUNKS * index(b) + half + 1)
                    pe.wait_ge(values_b_done, CHUNKS * index(b) + half + 1)
                pe.wait_ge(weight_hi_done, g + 1)

                def hi(it):
                    return pe.matmul(sums[:, it, 0:VCOLS], weight_hi[:, r, tile(it)], values[p][:, j],
                                     start=(j == 0), stop=(j == TILES - 1 and it >= HALF_TILES))

                def lo(i, it):
                    return pe.matmul(sums[:, it, CHANNELS:VCOLS], weight_lo[:, i % RING, tile(it)],
                                     values_b[p][:, i % TILES], start=False,
                                     stop=(i % TILES == TILES - 1 and it < HALF_TILES))

                def wait_lo(i):
                    pe.wait_ge(weight_lo_pool_done if i in POOL_STEPS else weight_lo_done, lo_count(b, i))

                if j < TILES - 1:
                    for it in range(CHUNK_TILES):
                        if j == 0 and it % HALF_TILES == 0:
                            wait(pe, sums_freed, HALVES * (CHUNKS * index(b) + h - 1) + it // HALF_TILES + 1)
                        hi(it)
                    if k % 2 == 1:
                        for i in (k - 1, k):
                            wait_lo(i)
                            for it in range(CHUNK_TILES):
                                last = lo(i, it)
                            last.then_inc(sums_step, 1)
                else:
                    for it in tiles_of_half(0):
                        hi(it)
                    wait_lo(k - 1)
                    wait_lo(k)
                    for i in (k - 1, k):
                        for it in tiles_of_half(0):
                            last = lo(i, it)
                    last.then_inc(sums_done, 1)
                    for i in (k - 1, k):
                        for it in tiles_of_half(1):
                            last = lo(i, it)
                        last.then_inc(sums_step, 1)
                    for it in tiles_of_half(1):
                        last = hi(it)
                    last.then_inc(sums_done, 1)

            def keep_busy(turns, place):
                for _ in range(turns):
                    pe.transpose(place[:, 0:128], identity[:, :], identity[:, :])

            pe.wait_ge(pool_setup, IDENTITY_MADE)
            keep_busy(WARM_UP[0], sums[:, 0])
            pe.wait_ge(w_qk_loaded, 2 * 16)
            pe.transpose(bank(0)[:, 0:128], w_qk[:, :], identity[:, :]).then_inc(w_turned, 1)
            keep_busy(WARM_UP[1], sums[:, 0])
            def project_first(name):
                h = int(name[1])
                place = scores[:, h] if name[0] == "k" else bank(h)
                pe.wait_ge(first_x_loaded[h], 16)
                pe.matmul(place, (w_kk_t if name[0] == "k" else w_qq_t)[:, :].rearrange("c a m -> c (a m)"),
                          x_sb[:, 0, chunk(h)], start=True, stop=True).then_inc(first_done, 1)

            for name in FIRST[:3]:
                pe.wait_ge(w_ready, 1 if name[0] == "k" else 3)
                project_first(name)
            pe.wait_ge(rest_loaded, 3 * 16)
            pe.transpose(bank(1)[:, 0:128], w_v[:, :], identity[:, :]).then_inc(w_turned, 1)
            pe.wait_ge(first_hi_done, FIRST.index("q0") + 1)
            pe.wait_ge(first_lo_done, FIRST_LO.index("k0") + 1)
            for t in range(CHUNK_TILES):
                max_scores(Batch(0, 0), t, 0, sums[:, t])
            pe.wait_ge(w_v_ready, 1)
            project_first(FIRST[3])
            pe.wait_ge(first_ones_done, CHUNKS)
            pe.wait_ge(first_lo_done, FIRST_LO.index("k1") + 1)
            for half in range(CHUNKS):
                for t in range(half * HALF_TILES, (half + 1) * HALF_TILES):
                    pe.wait_ge(neg_max_done, t + 1)
                    max_scores(Batch(0, 0), t, 1, sums[:, t])
                project_v(Batch(0, 0), half, scores[:, half])
            pe.wait_ge(neg_max_r_done, 1)
            pe.wait_ge(pool_setup, SETUP_MADE)
            turn_max(0, sums[:, 0])
            pe.wait_ge(first_lo_done, FIRST_LO.index("q0") + 1)
            pe.wait_ge(first_hi_done, len(FIRST))
            for k in range(AHEAD):
                pe.wait_ge(v_full_done, k + 1)
                score_tile(Batch(0, 0), k)

            def batch(b, has_prev, has_next):
                for k in range(STEPS):
                    first, ahead, behind = jobs_of(k, has_prev, has_next)
                    for job in first:
                        do_job(job, b, after(b), (b, (has_prev, has_next)))
                    if k + AHEAD < STEPS:
                        score_tile(b, k + AHEAD)
                    elif has_next:
                        score_tile(after(b), k + AHEAD - STEPS)
                    for job in ahead:
                        do_job(job, b, after(b), (b, (has_prev, has_next)))
                    weighted_sums(b, k)
                    for job in behind:
                        do_job(job, b, after(b), (b, (has_prev, has_next)))

            over_batches(pe, batch)
            wait_read_out(1, bank_order(1, all_jobs(True, False))[-1], LAST)
            pe.wait_ge(scaled_done, CHUNKS * index(LAST) + 1)
            turn_out(range(CHUNK_TILES), bank(1))
            for half in range(HALVES):
                pe.wait_ge(last_scaled, half + 1)
                turn_out(tiles_of_half(half), scores[:, half])

        @block.scalar
        def _(act):
            act.dma_start(w_qk[0:HEAD, :], Wq).then_inc(w_qk_loaded, 16)
            for half in range(2):
                act.dma_start(b_kk[half * HEAD:(half + 1) * HEAD, :],
                              bk.rearrange("(p a) -> p a", a=1)).then_inc(biases_loaded, 16)
            act.wait_ge(pool_setup, IDENTITY_MADE)
            act.activation(exp_of_identity[:, :], identity[:, 0:1], ACT.Exp)

            def round_qk(n, h, place):
                act.wait_ge(qk_done, qk_count(n, h))
                if h == 0:
                    m = before(n)
                    wait(act, spread_rest[m.parity], loads(m, SPREAD_REST))
                    wait(act, spread_mx[m.parity], loads(m, SPREAD_MX))
                act.activation(qk_hi[:, chunk(h)], place, ACT.Identity, bias=b_qk[:, :]).then_inc(qk_hi_done, 1)

            def round_x(n, h):
                wait_x(act, n)
                wait(act, qk_done, qk_count(before(n), h))
                act.activation(x_hi[:, chunk(h)], x_sb[:, n.parity, chunk(h)], ACT.Copy).then_inc(x_hi_done, 1)

            def take_v(n, half, place):
                c = CHUNKS * index(n) + half
                act.wait_ge(v_done, c + 1)
                wait(act, v_lo_done, c - 1)
                act.activation(v_full[:, half], place.rearrange("p (t c) -> p t c", c=CHANNELS),
                               ACT.Copy).then_inc(v_full_done, 1)

            def write_max_rows(n, h, place):
                act.wait_ge(mt_done, CHUNKS * index(n) + h + 1)
                done = act.activation(q_lomax[n.parity][HEAD:HEAD + 1, chunk(h)], place[0:1, :], ACT.Copy)
                done.then_inc(max_rows_done, 1)

            def do_job(job, b, n):
                if job in ("qk0_next", "qk1_next"):
                    round_qk(n, int(job[2]), bank(bank_of(job)))
                elif job in ("v0_next", "v1_next"):
                    take_v(n, int(job[1]), bank(bank_of(job)))
                elif job.startswith("mt"):
                    write_max_rows(n if job.endswith("_next") else b, int(job[2]), bank(bank_of(job)))

            def wait_low(b, k):
                act.wait_ge(weight_lo_pool_done if k in POOL_STEPS else weight_lo_done, lo_count(b, k))

            def exponentials(b, k):
                g, r = STEPS * index(b) + k, k % RING
                act.wait_ge(scores_done, g + 1)
                if k >= RING:
                    wait_low(b, k - RING)
                elif not isinstance(index(b), int) or index(b) > 0:
                    wait_low(before(b), k - RING + STEPS)
                act.activation(weight[:, r], scores[:, k % 2], ACT.Exp)
                wait(act, sums_step, g - RING + 1)
                act.activation(weight_hi[:, r], scores[:, k % 2], ACT.Exp).then_inc(weight_hi_done, 1)

            def take_low_sum(b, h):
                for half in range(HALVES):
                    c = HALVES * (CHUNKS * index(b) + h) + half
                    its = slice(half * HALF_TILES, (half + 1) * HALF_TILES)
                    act.wait_ge(sums_done, c + 1)
                    wait(act, sums_freed, c - HALVES + 1)
                    act.activation(low_sum[:, its, 0:CHANNELS], sums[:, its, 0:CHANNELS], ACT.Copy).then_inc(low_sum_done, 1)

            act.wait_ge(biases_loaded, 4 * 16)
            for i, name in enumerate(FIRST):
                h = int(name[1])
                act.wait_ge(first_done, i + 1)
                if name[0] == "k":
                    act.activation(k_hilo[0][:, chunk(h)], scores[:, h], ACT.Identity, bias=b_kk[:, :]).then_inc(first_hi_done, 1)
                else:
                    act.activation(q_hihi[0][:, chunk(h)], bank(h), ACT.Identity, bias=b_qq[:, :]).then_inc(first_hi_done, 1)
                if name == "k1":
                    act.wait_ge(w_turned, 2)
                    act.activation(w_v_t[:, :], bank(1)[:, 0:128], ACT.Copy).then_inc(w_v_ready, 1)
                    for i in range(CHUNKS):
                        act.activation(k_hione[0][0:HEAD, chunk(i)], scores[0:HEAD, i], ACT.Identity,
                                       bias=b_kk[0:HEAD, :]).then_inc(first_ones_done, 1)
            for half in range(CHUNKS):
                take_v(Batch(0, 0), half, scores[:, half])
            act.wait_ge(pool_setup, SETUP_MADE)
            write_max_rows(Batch(0, 0), 0, sums[:, 0])
            for k in range(AHEAD):
                exponentials(Batch(0, 0), k)

            def batch(b, has_prev, has_next):
                for k in range(STEPS):
                    if k == 0 and has_prev:
                        take_low_sum(before(b), 1)
                    if k == TILES:
                        take_low_sum(b, 0)
                    jobs = sum(jobs_of(k, has_prev, has_next), [])
                    for job in jobs:
                        if job in EARLY:
                            do_job(job, b, after(b))
                    if k + AHEAD < STEPS:
                        exponentials(b, k + AHEAD)
                    elif has_next:
                        exponentials(after(b), k + AHEAD - STEPS)
                    for job in jobs:
                        if job not in EARLY:
                            do_job(job, b, after(b))
                    for h in range(CHUNKS):
                        if k == X_HI[h] and has_next:
                            round_x(after(b), h)

            over_batches(act, batch)
            take_low_sum(LAST, 1)

        @block.vector
        def _(dve):
            def rest_of_x(b, h):
                dve.wait_ge(x_hi_done, qk_count(b, h))
                dve.tensor_tensor(x_lo[:, chunk(h)], x_sb[:, b.parity, chunk(h)], x_hi[:, chunk(h)],
                                   ALU.subtract).then_inc(x_lo_done, 1)

            def rest_of_qk(n, h, place):
                dve.wait_ge(qk_hi_done, qk_count(n, h))
                done = dve.scalar_tensor_tensor(qk_lo[:, chunk(h)], place, b_qk[:, :], qk_hi[:, chunk(h)],
                                                ALU.add, ALU.subtract)
                done.then_inc(qk_lo_done, 1)

            def maximum(t, h, place):
                dve.reduce_max(neg_max[:, h, t:t + 1], place, AX.X, negate=True).then_inc(neg_max_done, 1)

            def round_max(n, chunk_of):
                c = CHUNKS * index(n) + chunk_of
                cols = slice(chunk_of * CHUNK_TILES, (chunk_of + 1) * CHUNK_TILES)
                dve.wait_ge(neg_max_done, 2 * CHUNK_TILES * (c + 1))
                wait(dve, mt_done, c - 1)
                dve.tensor_tensor(neg_max_r[:, cols], neg_max[:, 0, cols], neg_max[:, 1, cols],
                                  ALU.min).then_inc(neg_max_r_done, 1)

            def finish(n, h, place):
                c = CHUNKS * index(n) + h
                dve.wait_ge(out_turned, c + 1)
                dve.wait_ge(x_bias_done, index(n) + 1)
                wait(dve, y_stored[h], 16 * index(n))
                done = dve.tensor_tensor(y_sb[:, h], place, x_bias[:, n.parity, chunk(h)], ALU.add)
                done.then_inc(y_done, 1)

            def do_job(job, b, n):
                if job in ("qk0_next", "qk1_next"):
                    rest_of_qk(n, int(job[2]), bank(bank_of(job)))
                elif job.startswith("mx"):
                    m, t, h = n if job.endswith("_next") else b, int(job[2]), "ab".index(job[3])
                    dve.wait_ge(mx_done, mx_count(m, job))
                    maximum(t, h, bank(h))
                    if t % CHUNK_TILES == CHUNK_TILES - 1 and h == 1:
                        round_max(m, t // CHUNK_TILES)
                elif job == "out_prev":
                    finish(before(b), 1, bank(bank_of(job)))
                elif job == "out_this":
                    finish(b, 0, bank(bank_of(job)))

            def low_weights(b, k):
                g, r = STEPS * index(b) + k, k % RING
                dve.wait_ge(weight_hi_done, g + 1)
                wait(dve, sums_step, g - RING + 1)
                dve.tensor_tensor(weight_lo[:, r], weight[:, r], weight_hi[:, r], ALU.subtract).then_inc(weight_lo_done, 1)

            def add_half(b, h, half):
                c = HALVES * (CHUNKS * index(b) + h) + half
                its = slice(half * HALF_TILES, (half + 1) * HALF_TILES)
                dve.wait_ge(low_sum_done, c + 1)
                if half == 0:
                    wait(dve, scaled_done, CHUNKS * index(b) + h)
                dve.tensor_tensor(total[:, its], sums[:, its, CHANNELS:2 * CHANNELS + 1], low_sum[:, its],
                                  ALU.add).then_inc(sums_freed, 1)

            def invert(b, h, first, last):
                its = slice(first * HALF_TILES, (last + 1) * HALF_TILES)
                dve.wait_ge(sums_freed, HALVES * (CHUNKS * index(b) + h) + last + 1)
                dve.reciprocal(one_over[:, its], total[:, its, CHANNELS]).then_inc(one_over_done, 1)

            def add_sums(b, h):
                for half in range(HALVES):
                    add_half(b, h, half)

            def turned_twice(cols):
                return bank(0)[:, cols].rearrange("c (a m) -> c a m", a=1).broadcast_to([CHANNELS, 2, HEAD])

            dve.wait_ge(w_turned, 1)
            dve.tensor_copy(w_kk_t[:, :], turned_twice(slice(HEAD, 2 * HEAD))).then_inc(w_ready, 1)
            dve.tensor_copy(w_qq_t[:, :], turned_twice(slice(0, HEAD))).then_inc(w_ready, 1)
            dve.tensor_copy(w_qk_t[:, :], bank(0)[:, 0:2 * HEAD]).then_inc(w_ready, 1)
            dve.wait_ge(biases_loaded, 4 * 16)
            dve.tensor_copy(b_qk[0:HEAD, :], b_qq[0:HEAD, :]).then_inc(b_ready, 1)
            dve.tensor_copy(b_qk[HEAD:2 * HEAD, :], b_kk[HEAD:2 * HEAD, :]).then_inc(b_ready, 1)

            def first_lo(name):
                h = int(name[1])
                dve.wait_ge(first_hi_done, FIRST.index(name) + 1)
                if name[0] == "k":
                    low = slice(HEAD, 2 * HEAD)
                    done = dve.scalar_tensor_tensor(k_hilo[0][low, chunk(h)], scores[low, h], b_kk[low, :],
                                                    k_hilo[0][low, chunk(h)], ALU.add, ALU.subtract)
                else:
                    done = dve.scalar_tensor_tensor(q_lomax[0][0:HEAD, chunk(h)], bank(h)[0:HEAD, :], b_qq[0:HEAD, :],
                                                    q_hihi[0][0:HEAD, chunk(h)], ALU.add, ALU.subtract)
                done.then_inc(first_lo_done, 1)

            def first_maximum(t, h):
                dve.wait_ge(mx_done, h * CHUNK_TILES + t + 1)
                maximum(t, h, sums[:, t])

            first_lo("k0")
            first_maximum(0, 0)
            first_maximum(1, 0)
            first_lo("k1")
            first_maximum(2, 0)
            first_maximum(3, 0)
            first_maximum(0, 1)
            for t in range(1, CHUNK_TILES):
                first_maximum(t, 1)
            round_max(Batch(0, 0), 0)
            first_lo("q0")
            first_lo("q1")
            low_weights(Batch(0, 0), 0)
            dve.wait_ge(pool_setup, SETUP_MADE)

            def batch(b, has_prev, has_next):
                for k in range(STEPS):
                    if k == 0 and has_prev:
                        add_sums(before(b), 1)
                    if k == TILES:
                        add_sums(b, 0)
                    jobs = sum(jobs_of(k, has_prev, has_next), [])
                    for job in jobs:
                        if job in DVE_EARLY:
                            do_job(job, b, after(b))
                    if k + 1 < STEPS:
                        if k + 1 not in POOL_STEPS:
                            low_weights(b, k + 1)
                    elif has_next and 0 not in POOL_STEPS:
                        low_weights(after(b), 0)
                    if k == 0 and has_prev:
                        invert(before(b), 1, 0, HALVES - 1)
                    if k == TILES:
                        invert(b, 0, 0, HALVES - 1)
                    for job in jobs:
                        if job not in DVE_EARLY:
                            do_job(job, b, after(b))
                    for h in range(CHUNKS):
                        if k == X_LO[h] and has_next:
                            rest_of_x(after(b), h)

            over_batches(dve, batch)
            h = CHUNKS - 1
            add_sums(LAST, h)
            dve.wait_ge(out_turned, CHUNKS * index(LAST) + 1)
            for half in range(HALVES):
                invert(LAST, h, half, half)
                dve.wait_ge(one_over_done, CHUNKS * index(LAST) + h + half + 1)
                for it in tiles_of_half(half):
                    done = dve.tensor_scalar(scaled[:, it], total[:, it, 0:CHANNELS], one_over[:, it:it + 1],
                                             gamma_col[:, :], ALU.mult, ALU.mult)
                done.then_inc(last_scaled, 1)
            finish(LAST, 0, bank(1))
            dve.wait_ge(y_stored[h], 16 * index(LAST))
            for half in range(HALVES):
                dve.wait_ge(out_turned, CHUNKS * index(LAST) + h + half + 1)
                cols = half_columns(half)
                done = dve.tensor_tensor(y_sb[:, h, cols], scores[:, half, cols], x_bias[:, LAST.parity, chunk(h)][:, cols],
                                         ALU.add)
                done.then_inc(y_done, 1)


_INS = ["x", "L0_conv_Wq", "L0_conv_bq", "L0_conv_Wk", "L0_conv_bk", "L0_conv_Wv", "L0_conv_bv", "L0_conv_gamma"]
_OUT = (BATCHES, CHANNELS, 32, 32)


def kernel(**inputs):
    import numpy as np
    import concourse.bacc as bacc
    from concourse.bass_utils import run_bass_kernel_spmd

    nc = bacc.Bacc("TRN2", target_bir_lowering=False, num_devices=1)
    arrays, args = {}, []
    for name in _INS:
        a = np.ascontiguousarray(inputs[name])
        arrays[f"in_{name}"] = a
        args.append(nc.dram_tensor(f"in_{name}", a.shape, mybir.dt.from_np(a.dtype), kind="ExternalInput").ap())
    args.append(nc.dram_tensor("out_0", _OUT, mybir.dt.float32, kind="ExternalOutput").ap())
    attention_program(nc, *args)
    result = run_bass_kernel_spmd(nc, [arrays], core_ids=[0])
    return result.results[0]["out_0"]
```
